# Optimizing a Trainium2 kernel written in Bass

```python
import numpy as np
import jax
import jax.numpy as jnp

def _softmax(x, axis=-1):
    return jax.nn.softmax(x, axis=axis)

def _gelu(x):
    return jax.nn.gelu(x, approximate=True)

def _silu(x):
    return jax.nn.silu(x)

def _sigmoid(x):
    return jax.nn.sigmoid(x)

def _layernorm(x, axis=-1, eps=1e-05):
    m = jnp.mean(x, axis=axis, keepdims=True)
    v = jnp.var(x, axis=axis, keepdims=True)
    return (x - m) / jnp.sqrt(v + eps)

def _scatter_add(tgt, idx, src, axis=0):
    return tgt.at[idx].add(src)

def _segment_sum(src, seg, n):
    return jax.ops.segment_sum(src, seg, n)
kernel_name = 'mk_cond_resid_d4_seqx_r4_19a4ab'

def setup_inputs(seed: int=0):
    np.random.seed(seed)
    _w = jnp.asarray

    def _rec_inputs():
        import jax
        import jax.numpy as jnp
        _rk = jax.random.key(seed)
        x = -7.109e-05 + 0.9999 * jax.random.normal(jax.random.fold_in(_rk, 1), (128, 64, 256), jnp.float32)
        _lenS = 64 - jax.random.randint(jax.random.fold_in(_rk, 7), (128,), 0, max(1, 64 // 4) + 1, jnp.int32)
        _lenS2 = 64 - jax.random.randint(jax.random.fold_in(_rk, 8), (128,), 0, max(1, 64 // 4) + 1, jnp.int32)
        itok_B_0_3 = jax.random.randint(jax.random.fold_in(_rk, 11), (128,), 0, 4, jnp.int32)
        itok_B_0_7 = jax.random.randint(jax.random.fold_in(_rk, 12), (128,), 0, 8, jnp.int32)
        itok_B_0_6 = jax.random.randint(jax.random.fold_in(_rk, 13), (128,), 0, 7, jnp.int32)
        return (x, itok_B_0_3, itok_B_0_7, itok_B_0_6)
    x, itok_B_0_3, itok_B_0_7, itok_B_0_6 = _rec_inputs()

    def _L0_cond_setup():
        import jax, jax.numpy as jnp
        import numpy as np
        D = 256
        RANK = 16
        ALPHA = 16.0
        SCALING = ALPHA / RANK
        N_LANG = 4
        B, S = (32, 512)
        key = jax.random.key(seed)
        k1, k2, k3, k4, k5 = jax.random.split(key, 5)
        x = jax.random.normal(k1, (B, S, D), dtype=jnp.float32)
        language_ids = jax.random.randint(k2, (B,), 0, N_LANG, dtype=jnp.int32)
        lora_A = jax.random.normal(k3, (N_LANG, RANK, D), dtype=jnp.float32) * 0.02
        lora_B = jax.random.normal(k4, (N_LANG, D, RANK), dtype=jnp.float32) * 0.02
        lang_embed = jax.random.normal(k5, (N_LANG, D), dtype=jnp.float32) * 0.02
        return {'x': x, 'language_ids': language_ids, 'lora_A': lora_A, 'lora_B': lora_B, 'lang_embed': lang_embed}
    _L0_cond_all = _L0_cond_setup()
    _L0_cond_in = {k: v for k, v in _L0_cond_all.items() if k in ('lora_A', 'lora_B', 'lang_embed')}
    del _L0_cond_all

    def _L1_cond_setup():
        import jax, jax.numpy as jnp
        import numpy as np
        B, S, D, F = (32, 128, 256, 1024)
        R_COMMON, R_DOMAIN, E = (16, 16, 8)
        ALPHA = 2.0

        def _expert_lora(x, expert_ids, Wa, Wb):
            Ab = Wa[expert_ids]
            Bb = Wb[expert_ids]
            low = jnp.einsum('bsd,brd->bsr', x, Ab)
            return ALPHA * jnp.einsum('bsr,bor->bso', low, Bb)
        key = jax.random.key(seed)
        ks = jax.random.split(key, 12)
        sd = lambda k, shape: jax.random.normal(k, shape, dtype=jnp.float32) * (1.0 / np.sqrt(shape[-1]))
        return {'hidden_states': jax.random.normal(ks[0], (B, S, D), dtype=jnp.float32), 'expert_ids': jax.random.randint(ks[1], (B,), 0, E, dtype=jnp.int32), 'wi': sd(ks[2], (F, D)), 'wo': sd(ks[3], (D, F)), 'common_wi_a': sd(ks[4], (R_COMMON, D)), 'common_wi_b': sd(ks[5], (F, R_COMMON)), 'common_wo_a': sd(ks[6], (R_COMMON, F)), 'common_wo_b': sd(ks[7], (D, R_COMMON)), 'experts_wi_a': sd(ks[8], (E, R_DOMAIN, D)), 'experts_wi_b': sd(ks[9], (F, R_DOMAIN)) * jnp.ones((E, 1, 1)) * 0.0 + sd(ks[9], (E, F, R_DOMAIN)), 'experts_wo_a': sd(ks[10], (E, R_DOMAIN, F)), 'experts_wo_b': sd(ks[11], (E, D, R_DOMAIN))}
    _L1_cond_all = _L1_cond_setup()
    _L1_cond_in = {k: v for k, v in _L1_cond_all.items() if k in ('wi', 'wo', 'common_wi_a', 'common_wi_b', 'common_wo_a', 'common_wo_b', 'experts_wi_a', 'experts_wi_b', 'experts_wo_a', 'experts_wo_b')}
    del _L1_cond_all

    def _L2_cond_setup():
        import jax, jax.numpy as jnp
        import numpy as np
        S, O, H = (8, 256, 256)
        B, N = (32, 128)
        key = jax.random.key(seed)
        k1, k2, k3, k4 = jax.random.split(key, 4)
        x = jax.random.normal(k1, (B, N, H), dtype=jnp.float32)
        subject_id = jax.random.randint(k2, (B,), 0, S)
        wbound = jnp.sqrt(2.0 / 6.0) * jnp.sqrt(3.0 / H)
        weight = jax.random.uniform(k3, (S, O, H), minval=-wbound, maxval=wbound, dtype=jnp.float32)
        bbound = 1.0 / jnp.sqrt(H)
        bias = jax.random.uniform(k4, (S, O), minval=-bbound, maxval=bbound, dtype=jnp.float32)
        return {'x': x, 'subject_id': subject_id, 'weight': weight, 'bias': bias}
    _L2_cond_all = _L2_cond_setup()
    _L2_cond_in = {k: v for k, v in _L2_cond_all.items() if k in ('weight', 'bias')}
    del _L2_cond_all

    def _L3_cond_setup():
        import jax, jax.numpy as jnp
        import numpy as np
        N_PROFILES = 8
        HIDDEN = 256
        BOTTLENECK = 128
        EPS = 1e-05
        key = jax.random.key(seed)
        ks = jax.random.split(key, 8)
        B, S, H, K, P = (16, 512, HIDDEN, BOTTLENECK, N_PROFILES)
        down_w = jax.random.normal(ks[0], (P, H, K), dtype=jnp.float32) * (1.0 / np.sqrt(H))
        down_b = jax.random.normal(ks[1], (P, K), dtype=jnp.float32) * 0.01
        up_w = jax.random.normal(ks[2], (P, K, H), dtype=jnp.float32) * (1.0 / np.sqrt(K))
        up_b = jax.random.normal(ks[3], (P, H), dtype=jnp.float32) * 0.01
        ln_g = jnp.ones((P, H), dtype=jnp.float32)
        ln_b = jnp.zeros((P, H), dtype=jnp.float32)
        hidden = jax.random.normal(ks[4], (B, S, H), dtype=jnp.float32)
        profile_ids = jax.random.randint(ks[5], (B,), 0, P)
        return {'hidden': hidden, 'profile_ids': profile_ids, 'down_w': down_w, 'down_b': down_b, 'up_w': up_w, 'up_b': up_b, 'ln_g': ln_g, 'ln_b': ln_b}
    _L3_cond_all = _L3_cond_setup()
    _L3_cond_in = {k: v for k, v in _L3_cond_all.items() if k in ('down_w', 'down_b', 'up_w', 'up_b', 'ln_g', 'ln_b')}
    del _L3_cond_all
    return {'x': x, 'itok_B_0_3': itok_B_0_3, 'itok_B_0_7': itok_B_0_7, 'itok_B_0_6': itok_B_0_6, 'L0_cond_lora_A': _L0_cond_in['lora_A'], 'L0_cond_lora_B': _L0_cond_in['lora_B'], 'L0_cond_lang_embed': _L0_cond_in['lang_embed'], 'L1_cond_wi': _L1_cond_in['wi'], 'L1_cond_wo': _L1_cond_in['wo'], 'L1_cond_common_wi_a': _L1_cond_in['common_wi_a'], 'L1_cond_common_wi_b': _L1_cond_in['common_wi_b'], 'L1_cond_common_wo_a': _L1_cond_in['common_wo_a'], 'L1_cond_common_wo_b': _L1_cond_in['common_wo_b'], 'L1_cond_experts_wi_a': _L1_cond_in['experts_wi_a'], 'L1_cond_experts_wi_b': _L1_cond_in['experts_wi_b'], 'L1_cond_experts_wo_a': _L1_cond_in['experts_wo_a'], 'L1_cond_experts_wo_b': _L1_cond_in['experts_wo_b'], 'L2_cond_weight': _L2_cond_in['weight'], 'L2_cond_bias': _L2_cond_in['bias'], 'L3_cond_down_w': _L3_cond_in['down_w'], 'L3_cond_down_b': _L3_cond_in['down_b'], 'L3_cond_up_w': _L3_cond_in['up_w'], 'L3_cond_up_b': _L3_cond_in['up_b'], 'L3_cond_ln_g': _L3_cond_in['ln_g'], 'L3_cond_ln_b': _L3_cond_in['ln_b']}

def reference(x, itok_B_0_3, itok_B_0_7, itok_B_0_6, L0_cond_lora_A, L0_cond_lora_B, L0_cond_lang_embed, L1_cond_wi, L1_cond_wo, L1_cond_common_wi_a, L1_cond_common_wi_b, L1_cond_common_wo_a, L1_cond_common_wo_b, L1_cond_experts_wi_a, L1_cond_experts_wi_b, L1_cond_experts_wo_a, L1_cond_experts_wo_b, L2_cond_weight, L2_cond_bias, L3_cond_down_w, L3_cond_down_b, L3_cond_up_w, L3_cond_up_b, L3_cond_ln_g, L3_cond_ln_b):
    import jax
    import jax.numpy as jnp

    def _L0_cond_ref(x, language_ids, lora_A, lora_B, lang_embed):
        import jax, jax.numpy as jnp
        import numpy as np
        D = 256
        RANK = 16
        ALPHA = 16.0
        SCALING = ALPHA / RANK
        N_LANG = 4
        B, S = (32, 512)
        A = lora_A[language_ids]
        Bm = lora_B[language_ids]
        emb = lang_embed[language_ids]
        t = jnp.einsum('bsd,brd->bsr', x, A)
        lora_out = jnp.einsum('bsr,bdr->bsd', t, Bm) * SCALING
        return lora_out + emb[:, None, :]

    def _L1_cond_ref(hidden_states, expert_ids, wi, wo, common_wi_a, common_wi_b, common_wo_a, common_wo_b, experts_wi_a, experts_wi_b, experts_wo_a, experts_wo_b):
        import jax, jax.numpy as jnp
        import numpy as np
        B, S, D, F = (32, 128, 256, 1024)
        R_COMMON, R_DOMAIN, E = (16, 16, 8)
        ALPHA = 2.0

        def _expert_lora(x, expert_ids, Wa, Wb):
            Ab = Wa[expert_ids]
            Bb = Wb[expert_ids]
            low = jnp.einsum('bsd,brd->bsr', x, Ab)
            return ALPHA * jnp.einsum('bsr,bor->bso', low, Bb)
        x = hidden_states
        hidden_i = jnp.einsum('bsd,fd->bsf', x, wi)
        hidden_i += ALPHA * jnp.einsum('bsr,fr->bsf', jnp.einsum('bsd,rd->bsr', x, common_wi_a), common_wi_b)
        hidden_i += _expert_lora(x, expert_ids, experts_wi_a, experts_wi_b)
        hidden_i = jax.nn.relu(hidden_i)
        hidden_o = jnp.einsum('bsf,df->bsd', hidden_i, wo)
        hidden_o += ALPHA * jnp.einsum('bsr,dr->bsd', jnp.einsum('bsf,rf->bsr', hidden_i, common_wo_a), common_wo_b)
        hidden_o += _expert_lora(hidden_i, expert_ids, experts_wo_a, experts_wo_b)
        return hidden_o

    def _L2_cond_ref(x, subject_id, weight, bias):
        import jax, jax.numpy as jnp
        import numpy as np
        S, O, H = (8, 256, 256)
        B, N = (32, 128)
        W = weight[subject_id]
        b = bias[subject_id]
        y = jnp.einsum('bnh,boh->bno', x, W) + b[:, None, :]
        return y

    def _L3_cond_ref(hidden, profile_ids, down_w, down_b, up_w, up_b, ln_g, ln_b):
        import jax, jax.numpy as jnp
        import numpy as np
        N_PROFILES = 8
        HIDDEN = 256
        BOTTLENECK = 128
        EPS = 1e-05
        Wd = down_w[profile_ids]
        bd = down_b[profile_ids][:, None]
        Wu = up_w[profile_ids]
        bu = up_b[profile_ids][:, None]
        g = ln_g[profile_ids][:, None]
        b = ln_b[profile_ids][:, None]
        z = jax.nn.relu(jnp.einsum('bsh,bhk->bsk', hidden, Wd) + bd)
        y = hidden + jnp.einsum('bsk,bkh->bsh', z, Wu) + bu
        mu = jnp.mean(y, axis=-1, keepdims=True)
        var = jnp.mean(jnp.square(y - mu), axis=-1, keepdims=True)
        return (y - mu) * jax.lax.rsqrt(var + EPS) * g + b
    x = x + _L0_cond_ref(x, itok_B_0_3, L0_cond_lora_A, L0_cond_lora_B, L0_cond_lang_embed)
    x = x + _L1_cond_ref(x, itok_B_0_7, L1_cond_wi, L1_cond_wo, L1_cond_common_wi_a, L1_cond_common_wi_b, L1_cond_common_wo_a, L1_cond_common_wo_b, L1_cond_experts_wi_a, L1_cond_experts_wi_b, L1_cond_experts_wo_a, L1_cond_experts_wo_b)
    x = x + _L2_cond_ref(x, itok_B_0_7, L2_cond_weight, L2_cond_bias)
    x = x + _L3_cond_ref(x, itok_B_0_6, L3_cond_down_w, L3_cond_down_b, L3_cond_up_w, L3_cond_up_b, L3_cond_ln_g, L3_cond_ln_b)
    return x

_drawn_inputs = setup_inputs


def setup_inputs(seed=0):
    import zlib

    import numpy as np

    out = dict(_drawn_inputs(seed))
    spreads = {'L3_cond_ln_g': (1.0, 0.6), 'L3_cond_ln_b': (0.0, 0.665)}
    factors = {'L2_cond_bias': 8.0, 'L3_cond_down_b': 200.0, 'L3_cond_up_b': 200.0}
    for name, (base, spread) in spreads.items():
        noise = np.random.default_rng([zlib.crc32(name.encode()), seed]).standard_normal(out[name].shape)
        drawn = base * np.exp(spread * noise) if base else spread * noise
        out[name] = jnp.asarray(drawn.astype(out[name].dtype))
    for name, factor in factors.items():
        out[name] = (out[name] * factor).astype(out[name].dtype)
    return out
```

```python
from contextlib import ExitStack

import concourse.bass as bass
from concourse import mybir

F32 = mybir.dt.float32
F32R = mybir.dt.float32r
I32 = mybir.dt.int32
ALU = mybir.AluOpType
ACT = mybir.ActivationFunctionType

P = 128
ROWS, SEQ, D = 128, 64, 256
TOKENS = ROWS * SEQ
KD = D // P
F = 1024
KF = F // P
RANK, LANGS, EXPERTS, PROFILES = 16, 4, 8, 8
BOTTLE = 128
ALPHA = 2.0
EPS = 1e-5
BR = 8
BT = BR * SEQ
BLOCKS = ROWS // BR
HR = BR // 2
HT = HR * SEQ
PAIRS = HR // 2
ADDS = 2 * D + BOTTLE
CHUNK = 1024


def build(nc, xT, lang, expert, profile, lang_emb, common_wi_a, common_wi_bT, common_wo_a, common_wo_bT,
          weights, sub_b, prof_adds, prof_g, out):
    ctx = ExitStack()
    with ctx:
        def sb(name, shape, dt=F32):
            return ctx.enter_context(nc.sbuf_tensor(name, shape, dt))

        def sem(name):
            return ctx.enter_context(nc.semaphore(name))

        w_small = sb("w_small", [P, 2, CHUNK], F32R)
        w_ewib = sb("w_ewib", [P, 2, F], F32R)
        w_wi = sb("w_wi", [P, 2, KD * F], F32R)
        w_ewoa = sb("w_ewoa", [P, 2, KF * P], F32R)
        w_wo = sb("w_wo", [P, 2, KF * D], F32R)
        w_sub = sb("w_sub", [P, 2, KD * EXPERTS * D], F32R)
        w_down = sb("w_down", [P, 2, KD * PROFILES * BOTTLE], F32R)
        w_up = sb("w_up", [P, 2, PROFILES * D], F32R)
        w_la = w_small[:, :, 0:2 * P].rearrange("p s (k m) -> p s k m", k=KD)
        w_lb = w_small[:, :, 256:512]
        w_ewia = w_small[:, :, 512:768].rearrange("p s (k m) -> p s k m", k=KD)
        w_ewob = w_small[:, :, 768:1024]

        ids = sb("ids", [1, 2 * ROWS], I32)
        id_bc = sb("id_bc", [P, 2, ROWS], I32)
        id_f = sb("id_f", [P, 2, ROWS])
        group_i = sb("group_i", [P, 4], I32)
        group = sb("group", [P, 4])
        mask = sb("mask", [P, 2, ROWS])
        hot = sb("hot", [LANGS, ROWS])
        emb = sb("emb", [LANGS, D])
        emb_cols = sb("emb_cols", [P, KD, ROWS])
        ident = sb("ident", [P, P])

        x_in = sb("x_in", [P, KD, BT])
        x1 = sb("x1", [P, 2, KD, BT])
        x1p = sb("x1p", [P, 2, 2, KD, BT], F32R)
        tf = sb("tf", [P, BT])
        t2f = sb("t2f", [P, BT])
        t0p = sb("t0p", [P, BT], F32R)
        t1p = sb("t1p", [P, 2, BT], F32R)
        t2p = sb("t2p", [P, 2, BT], F32R)
        hp = sb("hp", [P, 2, 2, BT], F32R)
        xpad = sb("xpad", [P, 2, KD, HR * P], F32R)
        zpad = sb("zpad", [P, 2, HR * P], F32R)
        x3 = sb("x3", [P, 2, PAIRS * D])
        y = sb("y", [P, 2, PAIRS * D])
        z = sb("z", [P, PAIRS * BOTTLE])
        sub_bias = sb("sub_bias", [P, PAIRS, D])
        adds = sb("adds", [P, PAIRS, ADDS])
        gains = sb("gains", [P, PAIRS, D])
        stats = sb("stats", [P, PAIRS, 6])
        mv = sb("mv", [P, 2, PAIRS, 2])
        rstd = sb("rstd", [P, 2, PAIRS])
        minus_half = sb("minus_half", [P, PAIRS])
        eps = sb("eps", [P, PAIRS])
        stage = x1[:, :, :, :].rearrange("p s k t -> p s (k t)")
        ca_i, cb_i = t2f[0:RANK, 0:D], y[0:RANK, :, :].rearrange("r s f -> r (s f)")
        ca_o, cb_o = x3[0:RANK, :, :].rearrange("r s f -> r (s f)"), tf[0:RANK, 0:D]

        banks = [ctx.enter_context(nc.psum_tensor(f"bank{i}", [P, 512], F32)) for i in range(8)]
        h_bank = banks[0:2]
        x2_bank = banks[2:4]
        t2_bank = banks[4]
        x3_bank = [banks[5], banks[7]]
        x3t_bank = [banks[6], banks[5]]
        z_bank = [banks[7], banks[7]]
        zt_bank = [banks[5], banks[5]]
        y_bank = [banks[6], banks[5]]
        t0_bank = banks[6]
        x1_bank = [banks[6], banks[7]]
        t1_bank = banks[6]

        ids_landed = sem("ids_landed")
        tables_landed = sem("tables_landed")
        common_landed = sem("common_landed")
        stage_landed = [sem("stage0_landed"), sem("stage1_landed")]
        chunk_split = sem("chunk_split")
        consts_made = sem("consts_made")
        ident_made = sem("ident_made")
        setup_v = sem("setup_v")
        masks_made = sem("masks_made")
        emb_psum = sem("emb_psum")
        emb_made = sem("emb_made")
        common_psum = sem("common_psum")
        common_added = sem("common_added")
        chunk_hi = sem("chunk_hi")
        x_landed, xh_ready, xl_ready, xe_ready = sem("x_landed"), sem("xh_ready"), sem("xl_ready"), sem("xe_ready")
        t0_psum, t0_masked, t0_hi, t0_lo = sem("t0_psum"), sem("t0_masked"), sem("t0_hi"), sem("t0_lo")
        x1_psum, x1_full, x1_hi, x1_lo = sem("x1_psum"), sem("x1_full"), sem("x1_hi"), sem("x1_lo")
        t1_psum, t1_masked, t1_hi, t1_lo = sem("t1_psum"), sem("t1_masked"), sem("t1_hi"), sem("t1_lo")
        h_psum, h_hi, h_lo, h_used = sem("h_psum"), sem("h_hi"), sem("h_lo"), sem("h_used")
        t2_psum, t2_masked, t2_hi, t2_lo = sem("t2_psum"), sem("t2_masked"), sem("t2_hi"), sem("t2_lo")
        x2_psum, x2_full, x2_hi, x2_lo = sem("x2_psum"), sem("x2_full"), sem("x2_hi"), sem("x2_lo")
        x3_psum, x3_rows = sem("x3_psum"), sem("x3_rows")
        x3t_psum, x3t_hi, x3t_lo = sem("x3t_psum"), sem("x3t_hi"), sem("x3t_lo")
        z_psum, z_rows = sem("z_psum"), sem("z_rows")
        zt_psum, zt_hi, zt_lo = sem("zt_psum"), sem("zt_hi"), sem("zt_lo")
        y_base, x3_base = sem("y_base"), sem("x3_base")
        y_psum, y_rows, y_stats, y_moments = sem("y_psum"), sem("y_rows"), sem("y_stats"), sem("y_moments")
        var_eps, y_rstd, y_norm, y_gained, out_rows = sem("var_eps"), sem("y_rstd"), sem("y_norm"), sem("y_gained"), sem("out_rows")
        bias_landed, adds_landed, gains_landed = sem("bias_landed"), sem("adds_landed"), sem("gains_landed")
        out_stored = [sem("out0_stored"), sem("out1_stored")]

        block = ctx.enter_context(nc.Block())

        N_CHUNKS = weights.shape[0]
        CHUNKS = ([(w_small, 0)] + [(w_ewib, 0)] + [(w_wi, CHUNK * k) for k in range(KD)] + [(w_ewoa, 0)]
                  + [(w_wo, CHUNK * c) for c in range(2)] + [(w_sub, CHUNK * c) for c in range(4)]
                  + [(w_down, CHUNK * c) for c in range(2)] + [(w_up, CHUNK * c) for c in range(2)])
        assert len(CHUNKS) == N_CHUNKS
        WI_CHUNKS, WO_CHUNKS, SUB_CHUNKS = (2, 3), (5, 6), (7, 8, 9, 10)

        def f32(ap):
            return ap.bitcast(F32)

        def rows_of(v):
            return v.rearrange("p k (r c) -> p k r c", c=SEQ)

        def pad_x(part):
            return xpad[:, part, :, :].rearrange("p k (r c) -> p k r c", c=P)[:, :, :, 0:SEQ]

        def pad_z(part):
            return zpad[:, part, :].rearrange("p (r c) -> p r c", c=P)[:, :, 0:SEQ]

        def first_block(n):
            return isinstance(n, int) and n == 0

        def steps(eng, step):
            step(-1, 1, False, False, True)
            step(0, 0, True, False, True)
            step(1, 1, True, True, True)
            with eng.Fori(1, BLOCKS // 2 - 1) as i:
                step(2 * i, 0, True, True, True)
                step(2 * i + 1, 1, True, True, True)
            step(BLOCKS - 2, 0, True, True, True)
            step(BLOCKS - 1, 1, True, True, False)
            step(BLOCKS, 0, False, True, False)

        @block.sync
        def _(sp):
            sp.dma_start(ids[0:1, 0:ROWS], expert).then_inc(ids_landed, 16)
            sp.dma_start(ids[0:1, ROWS:2 * ROWS], profile).then_inc(ids_landed, 16)
            sp.dma_start(stage[:, 0, :], weights[0]).then_inc(stage_landed[0], 16)
            sp.dma_start(id_bc[:, 0, :], lang.partition_broadcast(P)).then_inc(tables_landed, 16)
            sp.dma_start(id_bc[:, 1, :], expert.partition_broadcast(P)).then_inc(tables_landed, 16)
            sp.dma_start(emb[:, :], lang_emb).then_inc(tables_landed, 16)
            sp.dma_start(stage[:, 1, :], weights[1]).then_inc(stage_landed[1], 16)
            sp.dma_start(ca_i, common_wi_a).then_inc(common_landed, 16)
            sp.dma_start(cb_i, common_wi_bT).then_inc(common_landed, 16)
            sp.dma_start(ca_o, common_wo_a).then_inc(common_landed, 16)
            sp.dma_start(cb_o, common_wo_bT).then_inc(common_landed, 16)
            for c in range(2, N_CHUNKS):
                sp.wait_ge(chunk_split, c - 1)
                sp.dma_start(stage[:, c % 2, :], weights[c]).then_inc(stage_landed[c % 2], 16)
            sp.wait_ge(ids_landed, 32)

            def row_ids(base, row0):
                return [sp.value_load(ids[0:1, bass.ds(base + row0 + r, 1)], min_val=0, max_val=EXPERTS - 1)
                        for r in range(HR)]

            def step(n, par, main, tail, front):
                blk_t, blk_f = n - 1, n + 1
                if front:
                    if main:
                        sp.wait_ge(x1_full, 2 * blk_f)
                    sp.dma_start(x_in[:, :, :], xT[:, :, bass.ds(blk_f * BT, BT)]).then_inc(x_landed, 16)
                if tail:
                    for half in range(2):
                        done = 2 * blk_t + half
                        row0 = blk_t * BR + half * HR
                        es = row_ids(0, row0)
                        sp.wait_ge(x3_rows, done)
                        for r in range(HR):
                            q = slice((r % 2) * SEQ, (r % 2) * SEQ + SEQ)
                            sp.dma_start(sub_bias[q, r // 2, :],
                                         sub_b[bass.ds(es[r], 1), :].rearrange("a c -> (a c)").partition_broadcast(SEQ)).then_inc(bias_landed, 16)
                        ps = row_ids(ROWS, row0)
                        sp.wait_ge(x3_base, done)
                        sp.wait_ge(z_rows, done)
                        for r in range(HR):
                            q = slice((r % 2) * SEQ, (r % 2) * SEQ + SEQ)
                            sp.dma_start(adds[q, r // 2, :],
                                         prof_adds[bass.ds(ps[r], 1), :].rearrange("a c -> (a c)").partition_broadcast(SEQ)).then_inc(adds_landed, 16)
                        sp.wait_ge(y_gained, done)
                        for r in range(HR):
                            q = slice((r % 2) * SEQ, (r % 2) * SEQ + SEQ)
                            sp.dma_start(gains[q, r // 2, :],
                                         prof_g[bass.ds(ps[r], 1), :].rearrange("a c -> (a c)").partition_broadcast(SEQ)).then_inc(gains_landed, 16)
                        if half == 1:
                            store(blk_t, 0)
                    store(blk_t, 1)

            def store(blk, half):
                sp.wait_ge(out_rows, 2 * blk + half + 1)
                dst = out[bass.ds(blk * BT + half * HT, HT), :].rearrange("(t p) c -> p t c", p=P)
                sp.dma_start(dst, y[:, half, :].rearrange("p (t c) -> p t c", c=D)).then_inc(out_stored[half], 16)

            steps(sp, step)
            sp.wait_ge(out_stored[0], 16 * BLOCKS)
            sp.wait_ge(out_stored[1], 16 * BLOCKS)

        @block.tensor
        def _(pe):
            def mm3(bank, w, x, first, last, skip=False):
                nc.tensor.matmul(bank, w(0), x(0), start=first, stop=False, skip_group_check=skip)
                nc.tensor.matmul(bank, w(1), x(0), start=False, stop=False, skip_group_check=skip)
                return nc.tensor.matmul(bank, w(0), x(1), start=False, stop=last, skip_group_check=skip)

            pe.wait_ge(masks_made, 1)
            for k in range(KD):
                last = nc.tensor.matmul(t2_bank[:, k * ROWS:(k + 1) * ROWS], emb[:, k * P:(k + 1) * P], hot[:, :],
                                        start=True, stop=True)
            last.then_inc(emb_psum, 1)
            pe.wait_ge(common_landed, 64)
            for k in range(KD):
                for j in range(2):
                    last = nc.tensor.matmul(banks[2 * k + j][:, :], ca_i[:, k * P:(k + 1) * P],
                                            cb_i[:, j * 512:(j + 1) * 512], start=True, stop=True)
                last.then_inc(common_psum, 1)
            pe.wait_ge(emb_made, 1)
            for m in range(KF):
                last = nc.tensor.matmul(banks[4 + m // 2][:, (m % 2) * D:(m % 2) * D + D], ca_o[:, m * P:(m + 1) * P],
                                        cb_o, start=True, stop=True)
                if m % 4 == 3:
                    last.then_inc(common_psum, 1)
            pe.wait_ge(ids_landed, 32)
            pe.wait_ge(ident_made, 2)
            pe.wait_ge(consts_made, 2)

            def w_of(t, lo, n=P):
                return lambda part: t[:, part, lo:lo + n]

            def row_ids(base, row0):
                return [pe.value_load(ids[0:1, bass.ds(base + row0 + r, 1)], min_val=0, max_val=EXPERTS - 1)
                        for r in range(HR)]

            def hidden(n, par, m):
                if m >= 2 or not first_block(n):
                    pe.wait_ge(h_lo, 8 * n + m - 1)
                bank = h_bank[m % 2][:, :]
                if m == 0:
                    pe.wait_ge(x1_hi, n + 1)
                    pe.wait_ge(x1_lo, n + 1)
                for k in range(KD):
                    mm3(bank, w_of(w_wi, k * F + m * P), lambda part: x1p[:, par, part, k, :], k == 0, False)
                if m == 0:
                    pe.wait_ge(t1_hi, n + 1)
                    pe.wait_ge(t1_lo, n + 1)
                mm3(bank, w_of(w_ewib, m * P), lambda part: t1p[:, part, :], False, True).then_inc(h_psum, 1)

            def outputs(n, m):
                if m == 0:
                    pe.wait_ge(x2_full, 2 * n)
                    pe.wait_ge(t2_masked, n)
                pe.wait_ge(h_hi, 8 * n + m + 1)
                pe.wait_ge(h_lo, 8 * n + m + 1)
                hid = lambda part: hp[:, m % 2, part, :]
                mm3(t2_bank[:, :], w_of(w_ewoa, m * P), hid, m == 0, m == KF - 1)
                for k in range(KD):
                    last = mm3(x2_bank[k][:, :], w_of(w_wo, m * D + k * P), hid, m == 0, False)
                last.then_inc(h_used, 1)

            def t0(blk, par):
                if not first_block(blk):
                    pe.wait_ge(t1_masked, blk)
                pe.wait_ge(xh_ready, blk + 1)
                pe.wait_ge(xl_ready, blk + 1)
                for k in range(KD):
                    last = mm3(t0_bank[:, :], lambda part: w_la[:, part, k, :],
                               lambda part: x1p[:, par, part, k, :], k == 0, k == KD - 1)
                last.then_inc(t0_psum, 1)

            def x1_cols(blk):
                pe.wait_ge(t0_masked, blk + 1)
                pe.wait_ge(t0_hi, blk + 1)
                pe.wait_ge(t0_lo, blk + 1)
                for k in range(KD):
                    for part in range(2):
                        last = nc.tensor.matmul(x1_bank[k][:, :], w_lb[:, part, k * P:(k + 1) * P], t0p[:, :],
                                                start=part == 0, stop=part == 1)
                    last.then_inc(x1_psum, 1)

            def t1(blk, par):
                pe.wait_ge(x1_full, 2 * blk + 2)
                pe.wait_ge(x1_hi, blk + 1)
                pe.wait_ge(x1_lo, blk + 1)
                for k in range(KD):
                    last = mm3(t1_bank[:, :], lambda part: w_ewia[:, part, k, :],
                               lambda part: x1p[:, par, part, k, :], k == 0, k == KD - 1)
                last.then_inc(t1_psum, 1)

            def x2_cols(blk):
                pe.wait_ge(t2_hi, blk + 1)
                pe.wait_ge(t2_lo, blk + 1)
                for k in range(KD):
                    last = mm3(x2_bank[k][:, :], w_of(w_ewob, k * P), lambda part: t2p[:, part, :], False, True)
                last.then_inc(x2_psum, 1)

            def window(t, r):
                lo = r * P - (r % 2) * SEQ
                return lambda part: t(part)[:, lo:lo + P]

            def x3_of(blk, half):
                es = row_ids(0, blk * BR + half * HR)
                pe.wait_ge(x2_hi, 2 * blk + half + 1)
                pe.wait_ge(x2_lo, 2 * blk + half + 1)
                for r in range(HR):
                    bank = x3_bank[half][:, (r // 2) * D:(r // 2) * D + D]
                    for k in range(KD):
                        last = mm3(bank, window(lambda part: xpad[:, part, k, :], r),
                                   lambda part: w_sub[:, part, bass.ds(es[r] * D + k * EXPERTS * D, D)],
                                   r % 2 == 0 and k == 0, r % 2 == 1 and k == KD - 1)
                last.then_inc(x3_psum, 1)

            def x3t(blk, half):
                pe.wait_ge(x3_rows, 2 * blk + half + 1)
                for k in range(KD):
                    for t in range(PAIRS):
                        last = nc.tensor.transpose(x3t_bank[half][:, k * HT + t * P:k * HT + (t + 1) * P],
                                                   x3[:, half, t * D + k * P:t * D + (k + 1) * P], ident[:, :])
                last.then_inc(x3t_psum, 1)

            def z_of(blk, half):
                ps = row_ids(ROWS, blk * BR + half * HR)
                pe.wait_ge(x3t_hi, 2 * blk + half + 1)
                pe.wait_ge(x3t_lo, 2 * blk + half + 1)
                for r in range(HR):
                    bank = z_bank[half][:, (r // 2) * BOTTLE:(r // 2) * BOTTLE + BOTTLE]
                    for k in range(KD):
                        last = mm3(bank, window(lambda part: xpad[:, part, k, :], r),
                                   lambda part: w_down[:, part, bass.ds(ps[r] * BOTTLE + k * PROFILES * BOTTLE, BOTTLE)],
                                   r % 2 == 0 and k == 0, r % 2 == 1 and k == KD - 1)
                last.then_inc(z_psum, 1)
                return ps

            def zt(blk, half):
                pe.wait_ge(z_rows, 2 * blk + half + 1)
                for t in range(PAIRS):
                    last = nc.tensor.transpose(zt_bank[half][:, t * P:(t + 1) * P],
                                               z[:, t * BOTTLE:(t + 1) * BOTTLE], ident[:, :])
                last.then_inc(zt_psum, 1)

            def y_of(blk, half, ps):
                pe.wait_ge(zt_hi, 2 * blk + half + 1)
                pe.wait_ge(zt_lo, 2 * blk + half + 1)
                for r in range(HR):
                    last = mm3(y_bank[half][:, (r // 2) * D:(r // 2) * D + D],
                               window(lambda part: zpad[:, part, :], r),
                               lambda part: w_up[:, part, bass.ds(ps[r] * D, D)], r % 2 == 0, r % 2 == 1)
                last.then_inc(y_psum, 1)

            def step(n, par, main, tail, front):
                blk_t, blk_f = n - 1, n + 1
                if main:
                    hidden(n, par, 0)
                if tail:
                    outputs(blk_t, KF - 1)
                if main:
                    hidden(n, par, 1)
                if tail:
                    x2_cols(blk_t)
                if main:
                    outputs(n, 0)
                    hidden(n, par, 2)
                if tail:
                    pe.wait_ge(y_rows, 2 * blk_t)
                    x3_of(blk_t, 0)
                if main:
                    outputs(n, 1)
                if tail:
                    if main:
                        pe.wait_ge(t1_masked, n + 1)
                    x3t(blk_t, 0)
                if main:
                    hidden(n, par, 3)
                if tail:
                    if main:
                        pe.wait_ge(x1_full, 2 * n + 2)
                    ps = z_of(blk_t, 0)
                if main:
                    outputs(n, 2)
                if tail:
                    zt(blk_t, 0)
                if main:
                    hidden(n, par, 4)
                if tail:
                    y_of(blk_t, 0, ps)
                    x3_of(blk_t, 1)
                if main:
                    outputs(n, 3)
                if tail:
                    x3t(blk_t, 1)
                if front:
                    if tail:
                        pe.wait_ge(y_rows, 2 * blk_t + 1)
                    t0(blk_f, 1 - par)
                if main:
                    hidden(n, par, 5)
                if tail:
                    ps = z_of(blk_t, 1)
                if main:
                    outputs(n, 4)
                if tail:
                    zt(blk_t, 1)
                if main:
                    hidden(n, par, 6)
                if front:
                    x1_cols(blk_f)
                if tail:
                    y_of(blk_t, 1, ps)
                if main:
                    outputs(n, 5)
                    hidden(n, par, 7)
                if front:
                    t1(blk_f, 1 - par)
                if main:
                    outputs(n, 6)

            pe.wait_ge(chunk_split, N_CHUNKS)
            steps(pe, step)

        @block.scalar
        def _(act):
            def copy(dst, src, scale=1.0):
                return nc.scalar.activation(dst, src, ACT.Copy, scale=scale)

            act.wait_ge(emb_psum, 1)
            copy(emb_cols[:, :, :].rearrange("p k r -> p (k r)"), t2_bank[:, 0:KD * ROWS]).then_inc(emb_made, 1)
            for c, (dst, col) in enumerate(CHUNKS):
                if c in WI_CHUNKS + WO_CHUNKS + SUB_CHUNKS:
                    act.wait_ge(common_added, 1 + (WI_CHUNKS + WO_CHUNKS + SUB_CHUNKS).index(c))
                else:
                    act.wait_ge(stage_landed[c % 2], 16 * (c // 2 + 1))
                if c == 0:
                    copy(dst[:, 0, 0:768], stage[:, 0, 0:768])
                    copy(dst[:, 0, 768:1024], stage[:, 0, 768:1024], ALPHA).then_inc(chunk_hi, 1)
                else:
                    copy(dst[:, 0, col:col + CHUNK], stage[:, c % 2, :], ALPHA if c == 1 else 1.0).then_inc(chunk_hi, 1)

            def step(n, par, main, tail, front):
                blk_t, blk_f = n - 1, n + 1

                def h(m):
                    if m >= 2 or not first_block(n):
                        act.wait_ge(h_used, 8 * n + m - 1)
                    act.wait_ge(h_psum, 8 * n + m + 1)
                    nc.scalar.activation(hp[:, m % 2, 0, :], h_bank[m % 2][:, :], ACT.Relu).then_inc(h_hi, 1)

                def x2(half):
                    act.wait_ge(z_psum, 2 * blk_t + half)
                    act.wait_ge(x2_full, 2 * blk_t + 2)
                    copy(pad_x(0), rows_of(x1[:, 1 - par, :, half * HT:(half + 1) * HT])).then_inc(x2_hi, 1)

                def x3t(half):
                    act.wait_ge(x3t_psum, 2 * blk_t + half + 1)
                    copy(pad_x(0), rows_of(x3t_bank[half][:, :].rearrange("p (k t) -> p k t", k=KD))).then_inc(x3t_hi, 1)

                def zt(half):
                    act.wait_ge(y_psum, 2 * blk_t + half)
                    act.wait_ge(zt_psum, 2 * blk_t + half + 1)
                    nc.scalar.activation(pad_z(0), zt_bank[half][:, 0:HT].rearrange("p (r c) -> p r c", c=SEQ),
                                         ACT.Relu).then_inc(zt_hi, 1)

                if main:
                    h(0)
                if tail:
                    act.wait_ge(x2_psum, blk_t)
                    act.wait_ge(t2_masked, blk_t + 1)
                    copy(t2p[:, 0, :], t2f[:, :]).then_inc(t2_hi, 1)
                if main:
                    h(1)
                if tail:
                    x2(0)
                if front:
                    if main:
                        act.wait_ge(h_psum, 8 * n)
                    act.wait_ge(x_landed, 16 * blk_f + 16)
                    copy(x1p[:, 1 - par, 0, :, :].rearrange("p k t -> p (k t)"),
                         x_in[:, :, :].rearrange("p k t -> p (k t)")).then_inc(xh_ready, 1)
                if main:
                    h(2)
                if tail:
                    x3t(0)
                if main:
                    h(3)
                if tail:
                    x2(1)
                    zt(0)
                if main:
                    h(4)
                if tail:
                    x3t(1)
                if front:
                    if main:
                        act.wait_ge(x1_psum, 2 * blk_f)
                    act.wait_ge(t0_masked, blk_f + 1)
                    copy(t0p[:, :], tf[:, :]).then_inc(t0_hi, 1)
                if main:
                    h(5)
                if tail:
                    zt(1)
                if main:
                    h(6)
                if front:
                    act.wait_ge(x1_full, 2 * blk_f + 2)
                    copy(x1p[:, 1 - par, 0, :, :].rearrange("p k t -> p (k t)"),
                         x1[:, 1 - par, :, :].rearrange("p k t -> p (k t)")).then_inc(x1_hi, 1)
                if main:
                    h(7)
                if front:
                    if main:
                        act.wait_ge(h_psum, 8 * n + 8)
                    act.wait_ge(t1_masked, blk_f + 1)
                    copy(t1p[:, 0, :], tf[:, :]).then_inc(t1_hi, 1)

            steps(act, step)

        @block.vector
        def _(dve):
            V = nc.vector
            dve.wait_ge(consts_made, 1)
            V.memset(f32(xpad[:, :, :, :]), 0.0)
            V.memset(f32(zpad[:, :, :]), 0.0)
            V.memset(eps[:, :], EPS)
            V.memset(minus_half[:, :], -0.5).then_inc(consts_made, 1)
            V.tensor_scalar(group_i[:, 1:2], group_i[:, 2:3], 4, None, ALU.arith_shift_right).then_inc(setup_v, 1)
            dve.wait_ge(setup_v, 1)
            V.tensor_scalar(group_i[:, 0:1], group_i[:, 1:2], 3, None, ALU.bitwise_and).then_inc(setup_v, 1)
            dve.wait_ge(setup_v, 2)
            V.tensor_copy(group[:, 0:3], group_i[:, 0:3]).then_inc(setup_v, 1)
            dve.wait_ge(tables_landed, 48)
            V.tensor_copy(id_f[:, :, :], id_bc[:, :, :]).then_inc(setup_v, 1)
            dve.wait_ge(setup_v, 4)
            V.tensor_scalar(mask[:, 0, :], id_f[:, 0, :], group[:, 0:1], None, ALU.is_equal)
            V.tensor_scalar(mask[:, 1, :], id_f[:, 1, :], group[:, 1:2], None, ALU.is_equal)
            V.tensor_scalar(hot[:, :], id_f[0:LANGS, 0, :], group[0:LANGS, 2:3], None,
                            ALU.is_equal).then_inc(masks_made, 1)
            added = 0
            for c, (dst, col) in enumerate(CHUNKS):
                src = stage[:, c % 2, :]
                if c in WI_CHUNKS + WO_CHUNKS + SUB_CHUNKS:
                    dve.wait_ge(stage_landed[c % 2], 16 * (c // 2 + 1))
                    if c in WI_CHUNKS:
                        k = c - WI_CHUNKS[0]
                        dve.wait_ge(common_psum, k + 1)
                        parts = [banks[2 * k], banks[2 * k + 1]]
                    elif c in WO_CHUNKS:
                        q = c - WO_CHUNKS[0]
                        dve.wait_ge(common_psum, 3 + q)
                        parts = [banks[4 + 2 * q], banks[5 + 2 * q]]
                    if c in SUB_CHUNKS:
                        dve.wait_ge(ident_made, 2)
                        k = (c - SUB_CHUNKS[0]) // 2
                        diag = src.rearrange("p (e o) -> p e o", o=D)[:, :, k * P:(k + 1) * P]
                        last = V.tensor_tensor(diag, diag, ident[:, :].unsqueeze(1).broadcast_to([P, 4, P]), ALU.add)
                    else:
                        for j in range(2):
                            s = src[:, j * 512:(j + 1) * 512]
                            last = V.scalar_tensor_tensor(out=s, in0=parts[j][:, :], scalar=ALPHA, in1=s,
                                                          op0=ALU.mult, op1=ALU.add)
                    last.then_inc(common_added, 1)
                    added += 1
                    dve.wait_ge(common_added, added)
                dve.wait_ge(chunk_hi, c + 1)
                if c == 0:
                    V.tensor_tensor(dst[:, 1, 0:768], src[:, 0:768], f32(dst[:, 0, 0:768]), ALU.subtract)
                    last = V.scalar_tensor_tensor(out=dst[:, 1, 768:1024], in0=src[:, 768:1024], scalar=ALPHA,
                                                  in1=f32(dst[:, 0, 768:1024]), op0=ALU.mult, op1=ALU.subtract)
                else:
                    last = V.scalar_tensor_tensor(out=dst[:, 1, col:col + CHUNK], in0=src,
                                                  scalar=ALPHA if c == 1 else 1.0,
                                                  in1=f32(dst[:, 0, col:col + CHUNK]), op0=ALU.mult, op1=ALU.subtract)
                last.then_inc(chunk_split, 1)

            def step(n, par, main, tail, front):
                blk_t, blk_f = n - 1, n + 1

                def h(m):
                    dve.wait_ge(h_hi, 8 * n + m + 1)
                    if m == 7 and tail:
                        dve.wait_ge(y_stats, 2 * blk_t + 2)
                    V.scalar_tensor_tensor(out=hp[:, m % 2, 1, :], in0=h_bank[m % 2][:, :], scalar=0.0,
                                           in1=f32(hp[:, m % 2, 0, :]), op0=ALU.max, op1=ALU.subtract).then_inc(h_lo, 1)

                def masked(dst, bank, which, blk):
                    m = mask[:, which, bass.ds(blk * BR, BR)].unsqueeze(2).broadcast_to([P, BR, SEQ])
                    return V.tensor_tensor(dst.rearrange("p (r c) -> p r c", c=SEQ),
                                           bank[:, :].rearrange("p (r c) -> p r c", c=SEQ), m, ALU.mult)

                def x3_(half):
                    dve.wait_ge(x3_psum, 2 * blk_t + half + 1)
                    dve.wait_ge(bias_landed, 16 * HR * (2 * blk_t + half + 1))
                    dve.wait_ge(out_rows, 2 * blk_t)
                    V.tensor_tensor(x3[:, half, :], x3_bank[half][:, :],
                                    sub_bias[:, :, :].rearrange("p t c -> p (t c)"), ALU.add).then_inc(x3_rows, 1)

                def x3t(half):
                    dve.wait_ge(x3t_hi, 2 * blk_t + half + 1)
                    if half == 1:
                        dve.wait_ge(y_stats, 2 * blk_t + 1)
                    V.tensor_tensor(pad_x(1), rows_of(x3t_bank[half][:, :].rearrange("p (k t) -> p k t", k=KD)),
                                    f32(pad_x(0)), ALU.subtract).then_inc(x3t_lo, 1)

                def z_(half):
                    dve.wait_ge(z_psum, 2 * blk_t + half + 1)
                    dve.wait_ge(adds_landed, 16 * HR * (2 * blk_t + half + 1))
                    V.tensor_tensor(z[:, :].rearrange("p (t c) -> p t c", c=BOTTLE),
                                    z_bank[half][:, 0:PAIRS * BOTTLE].rearrange("p (t c) -> p t c", c=BOTTLE),
                                    adds[:, :, 2 * D:ADDS], ALU.add).then_inc(z_rows, 1)

                def zt(half):
                    dve.wait_ge(zt_hi, 2 * blk_t + half + 1)
                    V.scalar_tensor_tensor(out=pad_z(1), in0=zt_bank[half][:, 0:HT].rearrange("p (r c) -> p r c", c=SEQ),
                                           scalar=0.0, in1=f32(pad_z(0)), op0=ALU.max, op1=ALU.subtract).then_inc(zt_lo, 1)

                def y_(half):
                    dve.wait_ge(y_psum, 2 * blk_t + half + 1)
                    dve.wait_ge(y_base, 2 * blk_t + half + 1)
                    V.tensor_tensor(y[:, half, :], y_bank[half][:, :], y[:, half, :], ALU.add).then_inc(y_rows, 1)

                def stat(half):
                    dve.wait_ge(y_rows, 2 * blk_t + half + 1)
                    for t in range(PAIRS):
                        last = V.bn_stats(stats[:, t, :], y[:, half, t * D:(t + 1) * D])
                    last.then_inc(y_stats, 1)

                def aggregate(half):
                    if not main:
                        dve.wait_ge(y_stats, 2 * blk_t + half + 1)
                    for t in range(PAIRS):
                        last = V.bn_aggr(mv[:, half, t, :], stats[:, t, :])
                    last.then_inc(y_moments, 1)

                def normalize(half):
                    dve.wait_ge(y_rstd, 2 * blk_t + half + 1)
                    for t in range(PAIRS):
                        v = y[:, half, t * D:(t + 1) * D]
                        last = V.tensor_scalar(v, v, mv[:, half, t, 0:1], rstd[:, half, t:t + 1],
                                               ALU.subtract, ALU.mult)
                    last.then_inc(y_norm, 1)

                if main:
                    h(0)
                if tail:
                    dve.wait_ge(h_used, 8 * blk_t + 8)
                    dve.wait_ge(t2_lo, blk_t)
                    masked(t2f[:, :], t2_bank, 1, blk_t).then_inc(t2_masked, 1)
                if main:
                    h(1)
                if tail:
                    dve.wait_ge(x2_psum, blk_t + 1)
                    for k in range(KD):
                        V.tensor_tensor(x1[:, 1 - par, k, :], x2_bank[k][:, :], x1[:, 1 - par, k, :],
                                        ALU.add).then_inc(x2_full, 1)
                if main:
                    h(2)
                if tail:
                    x3_(0)
                    x3t(0)
                if main:
                    h(3)
                if tail:
                    z_(0)
                    zt(0)
                if main:
                    h(4)
                if tail:
                    y_(0)
                    x3_(1)
                    stat(0)
                    x3t(1)
                    aggregate(0)
                if front:
                    if main:
                        dve.wait_ge(t1_lo, blk_f)
                    dve.wait_ge(t0_psum, blk_f + 1)
                    masked(tf[:, :], t0_bank, 0, blk_f).then_inc(t0_masked, 1)
                if main:
                    h(5)
                if front:
                    dve.wait_ge(t0_hi, blk_f + 1)
                    V.tensor_tensor(t0p[SEQ:P, :], tf[SEQ:P, :], f32(t0p[SEQ:P, :]), ALU.subtract).then_inc(t0_lo, 1)
                if tail:
                    normalize(0)
                    z_(1)
                    zt(1)
                if main:
                    h(6)
                if front:
                    if tail:
                        dve.wait_ge(x2_hi, 2 * blk_t + 2)
                        dve.wait_ge(x2_lo, 2 * blk_t + 2)
                    dve.wait_ge(xe_ready, blk_f + 1)
                    for k in range(KD):
                        dve.wait_ge(x1_psum, 2 * blk_f + k + 1)
                        V.tensor_tensor(x1[:, 1 - par, k, :], x1_bank[k][:, :], x_in[:, k, :],
                                        ALU.add).then_inc(x1_full, 1)
                if tail:
                    y_(1)
                    stat(1)
                if main:
                    h(7)
                if tail:
                    aggregate(1)
                if front:
                    dve.wait_ge(t0_lo, blk_f + 1)
                    dve.wait_ge(t1_psum, blk_f + 1)
                    masked(tf[:, :], t1_bank, 1, blk_f).then_inc(t1_masked, 1)
                if tail:
                    normalize(1)

            dve.wait_ge(chunk_split, N_CHUNKS)
            steps(dve, step)

        @block.gpsimd
        def _(pool):
            G = nc.gpsimd
            G.iota(group_i[:, 2:3], pattern=[[0, 1]], base=0, channel_multiplier=1).then_inc(consts_made, 1)
            G.memset(ident[:, :], 0.0).then_inc(ident_made, 1)
            pool.wait_ge(ident_made, 1)
            G.affine_select(out=ident[:, :], in_=ident[:, :], compare_op=ALU.not_equal, fill=1.0, base=0,
                            pattern=[[-1, P]], channel_multiplier=1).then_inc(ident_made, 1)
            pool.wait_ge(emb_made, 1)
            pool.wait_ge(consts_made, 2)

            def step(n, par, main, tail, front):
                blk_t, blk_f = n - 1, n + 1

                def x2(half):
                    pool.wait_ge(x2_hi, 2 * blk_t + half + 1)
                    G.tensor_tensor(pad_x(1), rows_of(x1[:, 1 - par, :, half * HT:(half + 1) * HT]), f32(pad_x(0)),
                                    ALU.subtract).then_inc(x2_lo, 1)

                def base(half):
                    done = 2 * blk_t + half
                    pool.wait_ge(x3_rows, done + 1)
                    pool.wait_ge(adds_landed, 16 * HR * (done + 1))
                    pool.wait_ge(out_stored[half], 16 * blk_t)
                    x3v = x3[:, half, :].rearrange("p (t c) -> p t c", c=D)
                    G.tensor_tensor(y[:, half, :].rearrange("p (t c) -> p t c", c=D), x3v, adds[:, :, 0:D],
                                    ALU.add).then_inc(y_base, 1)
                    pool.wait_ge(x3t_psum, done + 1)
                    pool.wait_ge(y_base, done + 1)
                    G.tensor_tensor(x3v, x3v, adds[:, :, D:2 * D], ALU.add).then_inc(x3_base, 1)

                def inverse_deviation(half):
                    pool.wait_ge(y_moments, 2 * blk_t + half + 1)
                    G.tensor_tensor(rstd[:, half, :], mv[:, half, :, 1], eps[:, :], ALU.add).then_inc(var_eps, 1)
                    pool.wait_ge(var_eps, 2 * blk_t + half + 1)
                    G.tensor_tensor(rstd[:, half, :], rstd[:, half, :], minus_half[:, :], ALU.pow).then_inc(y_rstd, 1)

                def finish(half):
                    done = 2 * blk_t + half
                    pool.wait_ge(y_norm, done + 1)
                    pool.wait_ge(gains_landed, 16 * HR * (done + 1))
                    G.tensor_tensor(y[:, half, :], y[:, half, :], gains[:, :, :].rearrange("p t c -> p (t c)"),
                                    ALU.mult).then_inc(y_gained, 1)
                    pool.wait_ge(y_gained, done + 1)
                    pool.wait_ge(x3_base, done + 1)
                    G.tensor_tensor(y[:, half, :], y[:, half, :], x3[:, half, :], ALU.add).then_inc(out_rows, 1)

                if tail:
                    pool.wait_ge(t2_hi, blk_t + 1)
                    G.tensor_tensor(t2p[:, 1, :], t2f[:, :], f32(t2p[:, 0, :]), ALU.subtract).then_inc(t2_lo, 1)
                    x2(0)
                if front:
                    pool.wait_ge(xh_ready, blk_f + 1)
                    G.tensor_tensor(x1p[:, 1 - par, 1, :, :].rearrange("p k t -> p (k t)"),
                                    x_in[:, :, :].rearrange("p k t -> p (k t)"),
                                    f32(x1p[:, 1 - par, 0, :, :]).rearrange("p k t -> p (k t)"),
                                    ALU.subtract).then_inc(xl_ready, 1)
                    pool.wait_ge(xl_ready, blk_f + 1)
                    for k in range(KD):
                        e = emb_cols[:, k, bass.ds(blk_f * BR, BR)].unsqueeze(2).broadcast_to([P, BR, SEQ])
                        v = x_in[:, k, :].rearrange("p (r c) -> p r c", c=SEQ)
                        last = G.tensor_tensor(v, v, e, ALU.add)
                    last.then_inc(xe_ready, 1)
                if tail:
                    base(0)
                    x2(1)
                    base(1)
                if tail:
                    inverse_deviation(0)
                    finish(0)
                if front:
                    pool.wait_ge(x1_hi, blk_f + 1)
                    G.tensor_tensor(x1p[:, 1 - par, 1, :, :].rearrange("p k t -> p (k t)"),
                                    x1[:, 1 - par, :, :].rearrange("p k t -> p (k t)"),
                                    f32(x1p[:, 1 - par, 0, :, :]).rearrange("p k t -> p (k t)"),
                                    ALU.subtract).then_inc(x1_lo, 1)
                if tail:
                    inverse_deviation(1)
                if front:
                    pool.wait_ge(t1_hi, blk_f + 1)
                    G.tensor_tensor(t1p[:, 1, :], tf[:, :], f32(t1p[:, 0, :]), ALU.subtract).then_inc(t1_lo, 1)
                if tail:
                    finish(1)

            steps(pool, step)


def _layouts(i):
    import numpy as np
    c = np.ascontiguousarray
    tiles = lambda a: a.reshape(-1, P, a.shape[-1]).transpose(1, 0, 2).reshape(P, -1)
    la = i["L0_cond_lora_A"].reshape(LANGS * RANK, D).T
    la = np.concatenate([la, la], 1)
    lb = i["L0_cond_lora_B"].transpose(0, 2, 1).reshape(LANGS * RANK, D)
    lb = np.concatenate([lb, lb], 0)
    ewia = i["L1_cond_experts_wi_a"].reshape(EXPERTS * RANK, D).T
    ewib = i["L1_cond_experts_wi_b"].transpose(0, 2, 1).reshape(EXPERTS * RANK, F)
    ewoa = i["L1_cond_experts_wo_a"].reshape(EXPERTS * RANK, F).T
    ewob = i["L1_cond_experts_wo_b"].transpose(0, 2, 1).reshape(EXPERTS * RANK, D)
    sub = i["L2_cond_weight"].transpose(2, 0, 1).reshape(D, EXPERTS * D)
    down = i["L3_cond_down_w"].transpose(1, 0, 2).reshape(D, PROFILES * BOTTLE)
    up = i["L3_cond_up_w"].transpose(1, 0, 2).reshape(BOTTLE, PROFILES * D)
    w = np.concatenate([tiles(la), lb, tiles(ewia), ewob, ewib, tiles(i["L1_cond_wi"].T), tiles(ewoa),
                        tiles(i["L1_cond_wo"].T), tiles(sub), tiles(down), up], 1)
    w = w.reshape(P, -1, CHUNK).transpose(1, 0, 2)
    return {
        "xT": c(i["x"].reshape(TOKENS, KD, P).transpose(2, 1, 0)),
        "lang": c(i["itok_B_0_3"].reshape(ROWS)), "expert": c(i["itok_B_0_7"].reshape(ROWS)),
        "profile": c(i["itok_B_0_6"].reshape(ROWS)),
        "lang_emb": c(i["L0_cond_lang_embed"]),
        "common_wi_a": c(i["L1_cond_common_wi_a"]), "common_wi_bT": c(i["L1_cond_common_wi_b"].T),
        "common_wo_a": c(i["L1_cond_common_wo_a"]), "common_wo_bT": c(i["L1_cond_common_wo_b"].T),
        "weights": c(w), "sub_b": c(i["L2_cond_bias"]),
        "prof_adds": c(np.concatenate([i["L3_cond_up_b"], i["L3_cond_ln_b"], i["L3_cond_down_b"]], 1)),
        "prof_g": c(i["L3_cond_ln_g"]),
    }


def kernel(**inputs):
    import numpy as np
    import concourse.bacc as bacc
    from concourse.bass_utils import run_bass_kernel_spmd

    arrays = _layouts({k: np.asarray(v) for k, v in inputs.items()})
    nc = bacc.Bacc("TRN2", target_bir_lowering=False, num_devices=1)
    args = [nc.dram_tensor(f"in_{k}", a.shape, mybir.dt.from_np(a.dtype), kind="ExternalInput").ap()
            for k, a in arrays.items()]
    out = nc.dram_tensor("out_rows", (TOKENS, D), F32, kind="ExternalOutput").ap()
    build(nc, *args, out)
    r = run_bass_kernel_spmd(nc, [{f"in_{k}": a for k, a in arrays.items()}], core_ids=[0])
    return r.results[0]["out_rows"].reshape(ROWS, SEQ, D)
```

```python
from contextlib import ExitStack

import concourse.bass as bass
from concourse import mybir

F32 = mybir.dt.float32
F32R = mybir.dt.float32r
I32 = mybir.dt.int32
ALU = mybir.AluOpType
ACT = mybir.ActivationFunctionType

P = 128
ROWS, SEQ, D = 128, 64, 256
TOKENS = ROWS * SEQ
KD = D // P
F = 1024
KF = F // P
RANK, LANGS, EXPERTS, PROFILES = 16, 4, 8, 8
BOTTLE = 128
ALPHA = 2.0
EPS = 1e-5
BR = 8
BT = BR * SEQ
BLOCKS = ROWS // BR
HR = BR // 2
HT = HR * SEQ
PAIRS = HR // 2
ADDS = 2 * D + BOTTLE
CHUNK = 1024


def build(nc, xT, lang, expert, profile, lang_emb, common_wi_a, common_wi_bT, common_wo_a, common_wo_bT,
          weights, sub_b, prof_adds, prof_g, out):
    ctx = ExitStack()
    with ctx:
        def sb(name, shape, dt=F32):
            return ctx.enter_context(nc.sbuf_tensor(name, shape, dt))

        def sem(name):
            return ctx.enter_context(nc.semaphore(name))

        w_small = sb("w_small", [P, 2, CHUNK], F32R)
        w_ewib = sb("w_ewib", [P, 2, F], F32R)
        w_wi = sb("w_wi", [P, 2, KD * F], F32R)
        w_ewoa = sb("w_ewoa", [P, 2, KF * P], F32R)
        w_wo = sb("w_wo", [P, 2, KF * D], F32R)
        w_sub = sb("w_sub", [P, 2, KD * EXPERTS * D], F32R)
        w_down = sb("w_down", [P, KD, PROFILES, 2, BOTTLE], F32R)
        w_up = sb("w_up", [P, 2, PROFILES * D], F32R)
        w_la = w_small[:, :, 0:2 * P].rearrange("p s (k m) -> p s k m", k=KD)
        w_lb = w_small[:, :, 256:512]
        w_ewia = w_small[:, :, 512:768].rearrange("p s (k m) -> p s k m", k=KD)
        w_ewob = w_small[:, :, 768:1024]

        ids = sb("ids", [1, 2 * ROWS], I32)
        id_bc = sb("id_bc", [P, 2, ROWS], I32)
        id_f = sb("id_f", [P, 2, ROWS])
        group_i = sb("group_i", [P, 4], I32)
        group = sb("group", [P, 4])
        mask = sb("mask", [P, 2, ROWS])
        hot = sb("hot", [LANGS, ROWS])
        emb = sb("emb", [LANGS, D])
        emb_cols = sb("emb_cols", [P, KD, ROWS])
        ident = sb("ident", [P, P])

        x_in = sb("x_in", [P, KD, BT])
        x1 = sb("x1", [P, 2, KD, BT])
        x1p = sb("x1p", [P, 2, 2, KD, BT], F32R)
        tf = sb("tf", [P, BT])
        t2f = sb("t2f", [P, BT])
        t0p = sb("t0p", [P, BT], F32R)
        t1p = sb("t1p", [P, 2, BT], F32R)
        t2p = sb("t2p", [P, 2, BT], F32R)
        hp = sb("hp", [P, 2, 2, BT], F32R)
        xpad = sb("xpad", [P, 2, KD, HR * P], F32R)
        zpad = sb("zpad", [P, 2, HR * P], F32R)
        x3 = sb("x3", [P, 2, PAIRS * D])
        y = sb("y", [P, 2, PAIRS * D])
        z = sb("z", [P, PAIRS * BOTTLE])
        sub_bias = sb("sub_bias", [P, PAIRS, D])
        adds = sb("adds", [P, PAIRS, ADDS])
        gains = sb("gains", [P, PAIRS, D])
        stats = sb("stats", [P, PAIRS, 6])
        mv = sb("mv", [P, 2, PAIRS, 2])
        rstd = sb("rstd", [P, 2, PAIRS])
        minus_half = sb("minus_half", [P, PAIRS])
        eps = sb("eps", [P, PAIRS])
        stage = [t[:, :, :].rearrange("p s c -> p (s c)") for t in (y, x3)]
        ca_i, cb_i = t2f[0:RANK, 0:D], x1[0:RANK, 1, :, :].rearrange("r k t -> r (k t)")
        ca_o, cb_o = x1[32:32 + RANK, 1, :, :].rearrange("r k t -> r (k t)"), t2f[32:32 + RANK, D:2 * D]

        banks = [ctx.enter_context(nc.psum_tensor(f"bank{i}", [P, 512], F32)) for i in range(8)]
        h_bank = banks[0:2]
        x2_bank = banks[2:4]
        t2_bank = banks[4]
        x3_bank = [banks[5], banks[7]]
        x3t_bank = [banks[6], banks[5]]
        z_bank = [banks[7], banks[7]]
        zt_bank = [banks[5], banks[5]]
        y_bank = [banks[6], banks[5]]
        t0_bank = banks[6]
        x1_bank = [banks[6], banks[7]]
        t1_bank = banks[6]

        ids_landed = sem("ids_landed")
        tables_landed = sem("tables_landed")
        common_landed = sem("common_landed")
        stage_landed = [sem("stage0_landed"), sem("stage1_landed")]
        chunk_split = sem("chunk_split")
        consts_made = sem("consts_made")
        ident_made = sem("ident_made")
        setup_v = sem("setup_v")
        masks_made = sem("masks_made")
        emb_psum = sem("emb_psum")
        emb_made = sem("emb_made")
        common_psum = sem("common_psum")
        common_added = sem("common_added")
        chunk_hi = sem("chunk_hi")
        x_landed, xh_ready, xl_ready, xe_ready = sem("x_landed"), sem("xh_ready"), sem("xl_ready"), sem("xe_ready")
        t0_psum, t0_masked, t0_hi, t0_lo = sem("t0_psum"), sem("t0_masked"), sem("t0_hi"), sem("t0_lo")
        x1_psum, x1_full, x1_hi, x1_lo = sem("x1_psum"), sem("x1_full"), sem("x1_hi"), sem("x1_lo")
        t1_psum, t1_masked, t1_hi, t1_lo = sem("t1_psum"), sem("t1_masked"), sem("t1_hi"), sem("t1_lo")
        h_psum, h_hi, h_lo, h_used = sem("h_psum"), sem("h_hi"), sem("h_lo"), sem("h_used")
        t2_psum, t2_masked, t2_hi, t2_lo = sem("t2_psum"), sem("t2_masked"), sem("t2_hi"), sem("t2_lo")
        x2_psum, x2_full, x2_hi, x2_lo = sem("x2_psum"), sem("x2_full"), sem("x2_hi"), sem("x2_lo")
        x3_psum, x3_rows = sem("x3_psum"), sem("x3_rows")
        x3t_psum, x3t_hi, x3t_lo = sem("x3t_psum"), sem("x3t_hi"), sem("x3t_lo")
        z_psum, z_lo, z_rows = sem("z_psum"), sem("z_lo"), sem("z_rows")
        zt_psum, zt_hi, zt_lo = sem("zt_psum"), sem("zt_hi"), sem("zt_lo")
        y_base, x3_base = sem("y_base"), sem("x3_base")
        y_psum, y_rows, y_stats, y_moments = sem("y_psum"), sem("y_rows"), sem("y_stats"), sem("y_moments")
        var_eps, y_rstd, y_norm, y_gained, out_rows = sem("var_eps"), sem("y_rstd"), sem("y_norm"), sem("y_gained"), sem("out_rows")
        bias_landed, adds_landed, gains_landed = sem("bias_landed"), sem("adds_landed"), sem("gains_landed")
        out_stored = [sem("out0_stored"), sem("out1_stored")]

        block = ctx.enter_context(nc.Block())

        N_CHUNKS = weights.shape[0]

        def columns(t, c):
            return lambda part: t[:, part, c * CHUNK:(c + 1) * CHUNK]

        def wi_columns(j):
            return lambda part: w_wi[:, part, :].rearrange("p (k f) -> p k f", k=KD)[:, :, j * 512:(j + 1) * 512]

        def down_columns(k):
            return lambda part: w_down[:, k, :, part, :]

        CHUNKS = [columns(w_small, 0), columns(w_ewib, 0), wi_columns(0), columns(w_ewoa, 0), columns(w_wo, 0),
                  wi_columns(1), columns(w_wo, 1), *(columns(w_sub, c) for c in range(4)), down_columns(0),
                  down_columns(1), columns(w_up, 0), columns(w_up, 1)]
        assert len(CHUNKS) == N_CHUNKS
        EWIB, WI_CHUNKS, WO_CHUNKS, SUB_CHUNKS, DOWN_CHUNKS = 1, (2, 5), (4, 6), (7, 8, 9, 10), (11, 12)
        ADDED = (2, 4, 5, 6, 7, 8, 9, 10)
        COMMON_BANKS = {2: (0, 1), 4: (2, 3), 5: (5, 7), 6: (5, 7)}
        LATE = [(5,), (6,), (7,), (8,), (9,), (10,), (11, 12), (13, 14)]

        def staged(c):
            v = stage[c % 2]
            if c in WI_CHUNKS:
                return v.rearrange("p (k f) -> p k f", k=KD)
            return v.rearrange("p (e k) -> p e k", k=BOTTLE) if c in DOWN_CHUNKS else v

        def f32(ap):
            return ap.bitcast(F32)

        def rows_of(v):
            return v.rearrange("p k (r c) -> p k r c", c=SEQ)

        def pad_x(part):
            return xpad[:, part, :, :].rearrange("p k (r c) -> p k r c", c=P)[:, :, :, 0:SEQ]

        def pad_z(part):
            return zpad[:, part, :].rearrange("p (r c) -> p r c", c=P)[:, :, 0:SEQ]

        def row_ids(engine, base, row0):
            _, values = nc.values_load_multi_w_load_instructions(
                ids[0:1, bass.ds(base + row0, HR)], engines=(engine,), min_val=0, max_val=EXPERTS - 1,
                skip_runtime_bounds_check_because="an id names one of the tables' EXPERTS or PROFILES entries")
            return values

        def first_block(n):
            return isinstance(n, int) and n == 0

        def steps(eng, step):
            step(-1, 1, False, False, True)
            step(0, 0, True, False, True)
            step(1, 1, True, True, True)
            with eng.Fori(1, BLOCKS // 2 - 1) as i:
                step(2 * i, 0, True, True, True)
                step(2 * i + 1, 1, True, True, True)
            step(BLOCKS - 2, 0, True, True, True)
            step(BLOCKS - 1, 1, True, True, False)
            step(BLOCKS, 0, False, True, False)

        @block.sync
        def _(sp):
            sp.dma_start(ids[0:1, 0:ROWS], expert).then_inc(ids_landed, 16)
            sp.dma_start(ids[0:1, ROWS:2 * ROWS], profile).then_inc(ids_landed, 16)
            def load_chunk(c):
                if c >= 2:
                    sp.wait_ge(chunk_split, c - 1)
                sp.dma_start(stage[c % 2], weights[c]).then_inc(stage_landed[c % 2], 16)

            load_chunk(0)
            sp.dma_start(id_bc[:, 0, :], lang.partition_broadcast(P)).then_inc(tables_landed, 16)
            sp.dma_start(id_bc[:, 1, :], expert.partition_broadcast(P)).then_inc(tables_landed, 16)
            sp.dma_start(emb[:, :], lang_emb).then_inc(tables_landed, 16)
            load_chunk(1)
            def step(n, par, main, tail, front):
                blk_t, blk_f = n - 1, n + 1
                if front:
                    if main:
                        sp.wait_ge(x1_full, 2 * blk_f)
                    sp.dma_start(x_in[:, :, :], xT[:, :, bass.ds(blk_f * BT, BT)]).then_inc(x_landed, 16)
                if not tail and not main:
                    sp.dma_start(ca_i, common_wi_a).then_inc(common_landed, 16)
                    sp.dma_start(cb_i, common_wi_bT).then_inc(common_landed, 16)
                    sp.dma_start(ca_o, common_wo_a).then_inc(common_landed, 16)
                    sp.dma_start(cb_o, common_wo_bT).then_inc(common_landed, 16)
                    for c in range(2, 7):
                        load_chunk(c)
                    sp.wait_ge(ids_landed, 32)
                elif not tail:
                    for c in range(7, N_CHUNKS):
                        load_chunk(c)
                if tail:
                    for half in range(2):
                        done = 2 * blk_t + half
                        row0 = blk_t * BR + half * HR
                        es = row_ids(mybir.EngineType.SP, 0, row0)
                        sp.wait_ge(x3_rows, done)
                        for r in range(HR):
                            q = slice((r % 2) * SEQ, (r % 2) * SEQ + SEQ)
                            sp.dma_start(sub_bias[q, r // 2, :],
                                         sub_b[bass.ds(es[r], 1), :].rearrange("a c -> (a c)").partition_broadcast(SEQ)).then_inc(bias_landed, 16)
                        ps = row_ids(mybir.EngineType.SP, ROWS, row0)
                        sp.wait_ge(x3_base, done)
                        sp.wait_ge(z_rows, done)
                        for r in range(HR):
                            q = slice((r % 2) * SEQ, (r % 2) * SEQ + SEQ)
                            sp.dma_start(adds[q, r // 2, :],
                                         prof_adds[bass.ds(ps[r], 1), :].rearrange("a c -> (a c)").partition_broadcast(SEQ)).then_inc(adds_landed, 16)
                        sp.wait_ge(y_gained, done)
                        for r in range(HR):
                            q = slice((r % 2) * SEQ, (r % 2) * SEQ + SEQ)
                            sp.dma_start(gains[q, r // 2, :],
                                         prof_g[bass.ds(ps[r], 1), :].rearrange("a c -> (a c)").partition_broadcast(SEQ)).then_inc(gains_landed, 16)
                        if half == 1:
                            store(blk_t, 0)
                    store(blk_t, 1)

            def store(blk, half):
                sp.wait_ge(out_rows, 2 * blk + half + 1)
                dst = out[bass.ds(blk * BT + half * HT, HT), :].rearrange("(t p) c -> p t c", p=P)
                sp.dma_start(dst, y[:, half, :].rearrange("p (t c) -> p t c", c=D)).then_inc(out_stored[half], 16)

            steps(sp, step)
            sp.wait_ge(out_stored[0], 16 * BLOCKS)
            sp.wait_ge(out_stored[1], 16 * BLOCKS)

        @block.tensor
        def _(pe):
            def mm_hi(bank, w, x, first):
                nc.tensor.matmul(bank, w(0), x(0), start=first, stop=False)
                nc.tensor.matmul(bank, w(1), x(0), start=False, stop=False)

            def mm_lo(bank, w, x, last):
                return nc.tensor.matmul(bank, w(0), x(1), start=False, stop=last)

            def mm3(bank, w, x, first, last):
                mm_hi(bank, w, x, first)
                return mm_lo(bank, w, x, last)

            pe.wait_ge(masks_made, 1)
            for k in range(KD):
                last = nc.tensor.matmul(t2_bank[:, k * ROWS:(k + 1) * ROWS], emb[:, k * P:(k + 1) * P], hot[:, :],
                                        start=True, stop=True)
            last.then_inc(emb_psum, 1)

            def common(c):
                two = [banks[b] for b in COMMON_BANKS[c]]
                if c in WI_CHUNKS:
                    f = WI_CHUNKS.index(c) * 512
                    for k in range(KD):
                        last = nc.tensor.matmul(two[k][:, :], ca_i[:, k * P:(k + 1) * P], cb_i[:, f:f + 512],
                                                start=True, stop=True)
                else:
                    for q in range(4):
                        m = 4 * WO_CHUNKS.index(c) + q
                        last = nc.tensor.matmul(two[q // 2][:, (q % 2) * D:(q % 2) * D + D], ca_o[:, m * P:(m + 1) * P],
                                                cb_o, start=True, stop=True)
                last.then_inc(common_psum, 1)

            pe.wait_ge(common_landed, 64)
            common(2)
            common(4)
            pe.wait_ge(ids_landed, 32)
            pe.wait_ge(ident_made, 2)
            pe.wait_ge(consts_made, 2)

            def w_of(t, lo, n=P):
                return lambda part: t[:, part, lo:lo + n]

            def hidden(n, par, m):
                if m >= 2 or not first_block(n):
                    pe.wait_ge(h_lo, 8 * n + m - 1)
                bank = h_bank[m % 2][:, :]
                if first_block(n) and m in (0, 4):
                    pe.wait_ge(chunk_split, 6 if m else 3)
                for k in range(KD):
                    mm3(bank, w_of(w_wi, k * F + m * P), lambda part: x1p[:, par, part, k, :], k == 0, False)
                t1_of = lambda part: t1p[:, part, :]
                if m == 0:
                    pe.wait_ge(t1_hi, n + 1)
                mm_hi(bank, w_of(w_ewib, m * P), t1_of, False)
                if m == 0:
                    pe.wait_ge(t1_lo, n + 1)
                mm_lo(bank, w_of(w_ewib, m * P), t1_of, True).then_inc(h_psum, 1)

            def outputs(n, m):
                if first_block(n) and m in (0, 4):
                    pe.wait_ge(chunk_split, 7 if m else 5)
                if m == 0:
                    pe.wait_ge(x2_full, 2 * n)
                    pe.wait_ge(t2_masked, n)
                pe.wait_ge(h_hi, 8 * n + m + 1)
                pe.wait_ge(h_lo, 8 * n + m + 1)
                hid = lambda part: hp[:, m % 2, part, :]
                last = mm3(t2_bank[:, :], w_of(w_ewoa, m * P), hid, m == 0, m == KF - 1)
                if m == KF - 1:
                    last.then_inc(t2_psum, 1)
                for k in range(KD):
                    last = mm3(x2_bank[k][:, :], w_of(w_wo, m * D + k * P), hid, m == 0, False)
                last.then_inc(h_used, 1)

            def t0(blk, par):
                if first_block(blk):
                    pe.wait_ge(chunk_split, 1)
                else:
                    pe.wait_ge(t1_masked, blk)
                pe.wait_ge(xh_ready, blk + 1)
                pe.wait_ge(xl_ready, blk + 1)
                for k in range(KD):
                    last = mm3(t0_bank[:, :], lambda part: w_la[:, part, k, :],
                               lambda part: x1p[:, par, part, k, :], k == 0, k == KD - 1)
                last.then_inc(t0_psum, 1)

            def x1_cols(blk):
                pe.wait_ge(t0_masked, blk + 1)
                pe.wait_ge(t0_hi, blk + 1)
                pe.wait_ge(t0_lo, blk + 1)
                for k in range(KD):
                    for part in range(2):
                        last = nc.tensor.matmul(x1_bank[k][:, :], w_lb[:, part, k * P:(k + 1) * P], t0p[:, :],
                                                start=part == 0, stop=part == 1)
                    last.then_inc(x1_psum, 1)

            def t1(blk, par):
                pe.wait_ge(x1_full, 2 * blk + 2)
                pe.wait_ge(x1_hi, blk + 1)
                for k in range(KD):
                    mm_hi(t1_bank[:, :], lambda part: w_ewia[:, part, k, :], lambda part: x1p[:, par, part, k, :], k == 0)
                pe.wait_ge(x1_lo, blk + 1)
                for k in range(KD):
                    last = mm_lo(t1_bank[:, :], lambda part: w_ewia[:, part, k, :],
                                 lambda part: x1p[:, par, part, k, :], k == KD - 1)
                last.then_inc(t1_psum, 1)

            def x2_cols(blk):
                pe.wait_ge(t2_hi, blk + 1)
                for k in range(KD):
                    mm_hi(x2_bank[k][:, :], w_of(w_ewob, k * P), lambda part: t2p[:, part, :], False)
                pe.wait_ge(t2_lo, blk + 1)
                for k in range(KD):
                    last = mm_lo(x2_bank[k][:, :], w_of(w_ewob, k * P), lambda part: t2p[:, part, :], True)
                last.then_inc(x2_psum, 1)

            def window(t, r):
                lo = r * P - (r % 2) * SEQ
                return lambda part: t(part)[:, lo:lo + P]

            def x3_of(blk, half):
                es = row_ids(mybir.EngineType.PE, 0, blk * BR + half * HR)
                pe.wait_ge(x2_hi, 2 * blk + half + 1)
                pe.wait_ge(x2_lo, 2 * blk + half + 1)
                for r in range(HR):
                    bank = x3_bank[half][:, (r // 2) * D:(r // 2) * D + D]
                    for k in range(KD):
                        last = mm3(bank, window(lambda part: xpad[:, part, k, :], r),
                                   lambda part: w_sub[:, part, bass.ds(es[r] * D + k * EXPERTS * D, D)],
                                   r % 2 == 0 and k == 0, r % 2 == 1 and k == KD - 1)
                last.then_inc(x3_psum, 1)

            def x3t(blk, half):
                pe.wait_ge(x3_rows, 2 * blk + half + 1)
                for k in range(KD):
                    for t in range(PAIRS):
                        last = nc.tensor.transpose(x3t_bank[half][:, k * HT + t * P:k * HT + (t + 1) * P],
                                                   x3[:, half, t * D + k * P:t * D + (k + 1) * P], ident[:, :])
                last.then_inc(x3t_psum, 1)

            def z_of(blk, half):
                ps = row_ids(mybir.EngineType.PE, ROWS, blk * BR + half * HR)
                pe.wait_ge(x3t_hi, 2 * blk + half + 1)
                pe.wait_ge(x3t_lo, 2 * blk + half + 1)
                for r in range(HR):
                    bank = z_bank[half][:, (r // 2) * 2 * BOTTLE:(r // 2 + 1) * 2 * BOTTLE]
                    for k in range(KD):
                        both = w_down[:, k, :, :, :].rearrange("p e s k -> p (e s k)")[
                            :, bass.ds(ps[r] * 2 * BOTTLE, 2 * BOTTLE)]
                        for part in range(2):
                            last = nc.tensor.matmul(bank, window(lambda q: xpad[:, q, k, :], r)(part), both,
                                                    start=r % 2 == 0 and k == 0 and part == 0,
                                                    stop=r % 2 == 1 and k == KD - 1 and part == 1)
                last.then_inc(z_psum, 1)
                return ps

            def zt(blk, half):
                pe.wait_ge(z_rows, 2 * blk + half + 1)
                for t in range(PAIRS):
                    last = nc.tensor.transpose(zt_bank[half][:, t * P:(t + 1) * P],
                                               z[:, t * BOTTLE:(t + 1) * BOTTLE], ident[:, :])
                last.then_inc(zt_psum, 1)

            def y_of(blk, half, ps):
                pe.wait_ge(zt_hi, 2 * blk + half + 1)
                pe.wait_ge(zt_lo, 2 * blk + half + 1)
                for r in range(HR):
                    last = mm3(y_bank[half][:, (r // 2) * D:(r // 2) * D + D],
                               window(lambda part: zpad[:, part, :], r),
                               lambda part: w_up[:, part, bass.ds(ps[r] * D, D)], r % 2 == 0, r % 2 == 1)
                last.then_inc(y_psum, 1)

            def step(n, par, main, tail, front):
                blk_t, blk_f = n - 1, n + 1
                if first_block(n):
                    common(5)
                if main:
                    hidden(n, par, 0)
                if tail:
                    outputs(blk_t, KF - 1)
                if main:
                    hidden(n, par, 1)
                if tail:
                    x2_cols(blk_t)
                if main:
                    hidden(n, par, 2)
                    if first_block(n):
                        pe.wait_ge(common_added, 3)
                        common(6)
                    outputs(n, 0)
                if tail:
                    if first_block(blk_t):
                        pe.wait_ge(chunk_split, N_CHUNKS)
                    pe.wait_ge(y_rows, 2 * blk_t)
                    x3_of(blk_t, 0)
                if main:
                    outputs(n, 1)
                if tail:
                    if main:
                        pe.wait_ge(t1_masked, n + 1)
                    x3t(blk_t, 0)
                if main:
                    hidden(n, par, 3)
                if tail:
                    if main:
                        pe.wait_ge(x1_full, 2 * n + 2)
                    ps = z_of(blk_t, 0)
                if main:
                    outputs(n, 2)
                if tail:
                    zt(blk_t, 0)
                if main:
                    hidden(n, par, 4)
                if tail:
                    y_of(blk_t, 0, ps)
                    x3_of(blk_t, 1)
                if main:
                    outputs(n, 3)
                if tail:
                    x3t(blk_t, 1)
                if front:
                    if tail:
                        pe.wait_ge(y_rows, 2 * blk_t + 1)
                    t0(blk_f, 1 - par)
                if main:
                    hidden(n, par, 5)
                if tail:
                    ps = z_of(blk_t, 1)
                if main:
                    outputs(n, 4)
                if tail:
                    zt(blk_t, 1)
                if main:
                    hidden(n, par, 6)
                if front:
                    x1_cols(blk_f)
                if tail:
                    y_of(blk_t, 1, ps)
                if main:
                    outputs(n, 5)
                    hidden(n, par, 7)
                if front:
                    t1(blk_f, 1 - par)
                if main:
                    outputs(n, 6)

            steps(pe, step)

        @block.scalar
        def _(act):
            def copy(dst, src, scale=1.0):
                return nc.scalar.activation(dst, src, ACT.Copy, scale=scale)

            def split_hi(c):
                if c in ADDED:
                    act.wait_ge(common_added, 1 + ADDED.index(c))
                else:
                    act.wait_ge(stage_landed[c % 2], 16 * (c // 2 + 1))
                dst = CHUNKS[c]
                if c == 0:
                    copy(dst(0)[:, 0:768], stage[0][:, 0:768])
                    copy(dst(0)[:, 768:1024], stage[0][:, 768:1024], ALPHA).then_inc(chunk_hi, 1)
                else:
                    copy(dst(0), staged(c), ALPHA if c == EWIB else 1.0).then_inc(chunk_hi, 1)

            split_hi(0)
            act.wait_ge(emb_psum, 1)
            copy(emb_cols[:, :, :].rearrange("p k r -> p (k r)"), t2_bank[:, 0:KD * ROWS]).then_inc(emb_made, 1)

            def step(n, par, main, tail, front):
                blk_t, blk_f = n - 1, n + 1

                def h(m):
                    if m >= 2 or not first_block(n):
                        act.wait_ge(h_used, 8 * n + m - 1)
                    act.wait_ge(h_psum, 8 * n + m + 1)
                    nc.scalar.activation(hp[:, m % 2, 0, :], h_bank[m % 2][:, :], ACT.Relu).then_inc(h_hi, 1)
                    if first_block(n):
                        for c in LATE[m]:
                            split_hi(c)

                def x2(half):
                    act.wait_ge(z_psum, 2 * blk_t + half)
                    act.wait_ge(x2_full, 2 * blk_t + 2)
                    copy(pad_x(0), rows_of(x1[:, 1 - par, :, half * HT:(half + 1) * HT])).then_inc(x2_hi, 1)

                def x3t(half):
                    act.wait_ge(x3t_psum, 2 * blk_t + half + 1)
                    copy(pad_x(0), rows_of(x3t_bank[half][:, :].rearrange("p (k t) -> p k t", k=KD))).then_inc(x3t_hi, 1)

                def zt(half):
                    act.wait_ge(y_psum, 2 * blk_t + half)
                    act.wait_ge(zt_psum, 2 * blk_t + half + 1)
                    nc.scalar.activation(pad_z(0), zt_bank[half][:, 0:HT].rearrange("p (r c) -> p r c", c=SEQ),
                                         ACT.Relu).then_inc(zt_hi, 1)

                if main:
                    h(0)
                if tail:
                    act.wait_ge(x2_psum, blk_t)
                    act.wait_ge(t2_masked, blk_t + 1)
                    copy(t2p[:, 0, :], t2f[:, :]).then_inc(t2_hi, 1)
                if main:
                    h(1)
                if tail:
                    x2(0)
                if front:
                    if main:
                        act.wait_ge(h_psum, 8 * n)
                    act.wait_ge(x_landed, 16 * blk_f + 16)
                    copy(x1p[:, 1 - par, 0, :, :].rearrange("p k t -> p (k t)"),
                         x_in[:, :, :].rearrange("p k t -> p (k t)")).then_inc(xh_ready, 1)
                    if not main:
                        split_hi(1)
                if main:
                    h(2)
                if tail:
                    x3t(0)
                if main:
                    h(3)
                if tail:
                    x2(1)
                    zt(0)
                if main:
                    h(4)
                if tail:
                    x3t(1)
                if front:
                    if main:
                        act.wait_ge(x1_psum, 2 * blk_f)
                    act.wait_ge(t0_masked, blk_f + 1)
                    copy(t0p[:, :], tf[:, :]).then_inc(t0_hi, 1)
                    if not main:
                        split_hi(2)
                        split_hi(3)
                if main:
                    h(5)
                if tail:
                    zt(1)
                if main:
                    h(6)
                if front:
                    act.wait_ge(x1_full, 2 * blk_f + 2)
                    copy(x1p[:, 1 - par, 0, :, :].rearrange("p k t -> p (k t)"),
                         x1[:, 1 - par, :, :].rearrange("p k t -> p (k t)")).then_inc(x1_hi, 1)
                    if not main:
                        split_hi(4)
                if main:
                    h(7)
                if front:
                    if main:
                        act.wait_ge(h_psum, 8 * n + 8)
                    act.wait_ge(t1_masked, blk_f + 1)
                    copy(t1p[:, 0, :], tf[:, :]).then_inc(t1_hi, 1)

            steps(act, step)

        @block.vector
        def _(dve):
            V = nc.vector
            dve.wait_ge(consts_made, 1)
            V.memset(f32(xpad[:, :, :, :]), 0.0)
            V.memset(f32(zpad[:, :, :]), 0.0)
            V.memset(eps[:, :], EPS)
            V.memset(minus_half[:, :], -0.5).then_inc(consts_made, 1)
            V.tensor_scalar(group_i[:, 1:2], group_i[:, 2:3], 4, None, ALU.arith_shift_right).then_inc(setup_v, 1)
            dve.wait_ge(setup_v, 1)
            V.tensor_scalar(group_i[:, 0:1], group_i[:, 1:2], 3, None, ALU.bitwise_and).then_inc(setup_v, 1)
            dve.wait_ge(setup_v, 2)
            V.tensor_copy(group[:, 0:3], group_i[:, 0:3]).then_inc(setup_v, 1)
            dve.wait_ge(tables_landed, 48)
            V.tensor_copy(id_f[:, :, :], id_bc[:, :, :]).then_inc(setup_v, 1)
            dve.wait_ge(setup_v, 4)
            V.tensor_scalar(mask[:, 0, :], id_f[:, 0, :], group[:, 0:1], None, ALU.is_equal)
            V.tensor_scalar(mask[:, 1, :], id_f[:, 1, :], group[:, 1:2], None, ALU.is_equal)
            V.tensor_scalar(hot[:, :], id_f[0:LANGS, 0, :], group[0:LANGS, 2:3], None,
                            ALU.is_equal).then_inc(masks_made, 1)

            def add_to(c):
                dve.wait_ge(stage_landed[c % 2], 16 * (c // 2 + 1))
                src = stage[c % 2]
                if c in SUB_CHUNKS:
                    dve.wait_ge(ident_made, 2)
                    k = (c - SUB_CHUNKS[0]) // 2
                    diag = src.rearrange("p (e o) -> p e o", o=D)[:, :, k * P:(k + 1) * P]
                    last = V.tensor_tensor(diag, diag, ident[:, :].unsqueeze(1).broadcast_to([P, 4, P]), ALU.add)
                else:
                    dve.wait_ge(common_psum, 1 + ADDED.index(c))
                    for j, bank in enumerate(COMMON_BANKS[c]):
                        v = src[:, j * 512:(j + 1) * 512]
                        last = V.scalar_tensor_tensor(out=v, in0=banks[bank][:, :], scalar=ALPHA, in1=v,
                                                      op0=ALU.mult, op1=ALU.add)
                last.then_inc(common_added, 1)

            def split_lo(c):
                dve.wait_ge(chunk_hi, c + 1)
                src, dst = stage[c % 2], CHUNKS[c]
                if c == 0:
                    V.tensor_tensor(dst(1)[:, 0:768], src[:, 0:768], f32(dst(0))[:, 0:768], ALU.subtract)
                    last = V.scalar_tensor_tensor(out=dst(1)[:, 768:1024], in0=src[:, 768:1024], scalar=ALPHA,
                                                  in1=f32(dst(0))[:, 768:1024], op0=ALU.mult, op1=ALU.subtract)
                else:
                    last = V.scalar_tensor_tensor(out=dst(1), in0=staged(c), scalar=ALPHA if c == EWIB else 1.0,
                                                  in1=f32(dst(0)), op0=ALU.mult, op1=ALU.subtract)
                last.then_inc(chunk_split, 1)

            split_lo(0)

            def step(n, par, main, tail, front):
                blk_t, blk_f = n - 1, n + 1

                def h(m):
                    dve.wait_ge(h_hi, 8 * n + m + 1)
                    if m == 7 and tail:
                        dve.wait_ge(y_stats, 2 * blk_t + 2)
                    V.scalar_tensor_tensor(out=hp[:, m % 2, 1, :], in0=h_bank[m % 2][:, :], scalar=0.0,
                                           in1=f32(hp[:, m % 2, 0, :]), op0=ALU.max, op1=ALU.subtract).then_inc(h_lo, 1)
                    if first_block(n):
                        for c in LATE[m - 1] if m else ():
                            split_lo(c)
                        for c in LATE[m]:
                            if c in ADDED:
                                add_to(c)

                def masked(dst, bank, which, blk):
                    m = mask[:, which, bass.ds(blk * BR, BR)].unsqueeze(2).broadcast_to([P, BR, SEQ])
                    return V.tensor_tensor(dst.rearrange("p (r c) -> p r c", c=SEQ),
                                           bank[:, :].rearrange("p (r c) -> p r c", c=SEQ), m, ALU.mult)

                def x2lo(half):
                    dve.wait_ge(x2_hi, 2 * blk_t + half + 1)
                    V.tensor_tensor(pad_x(1), rows_of(x1[:, 1 - par, :, half * HT:(half + 1) * HT]), f32(pad_x(0)),
                                    ALU.subtract).then_inc(x2_lo, 1)

                def x3_(half):
                    dve.wait_ge(x3_psum, 2 * blk_t + half + 1)
                    dve.wait_ge(bias_landed, 16 * HR * (2 * blk_t + half + 1))
                    dve.wait_ge(out_rows, 2 * blk_t)
                    V.tensor_tensor(x3[:, half, :], x3_bank[half][:, :],
                                    sub_bias[:, :, :].rearrange("p t c -> p (t c)"), ALU.add).then_inc(x3_rows, 1)

                def x3t(half):
                    dve.wait_ge(x3t_hi, 2 * blk_t + half + 1)
                    if half == 1:
                        dve.wait_ge(y_stats, 2 * blk_t + 1)
                    V.tensor_tensor(pad_x(1), rows_of(x3t_bank[half][:, :].rearrange("p (k t) -> p k t", k=KD)),
                                    f32(pad_x(0)), ALU.subtract).then_inc(x3t_lo, 1)

                def z_(half):
                    dve.wait_ge(z_psum, 2 * blk_t + half + 1)
                    dve.wait_ge(adds_landed, 16 * HR * (2 * blk_t + half + 1))
                    zv = z[:, :].rearrange("p (t c) -> p t c", c=BOTTLE)
                    sums = z_bank[half][:, :].rearrange("p (t s c) -> p t s c", s=2, c=BOTTLE)
                    V.tensor_tensor(zv, sums[:, :, 1, :], adds[:, :, 2 * D:ADDS], ALU.add).then_inc(z_lo, 1)
                    dve.wait_ge(z_lo, 2 * blk_t + half + 1)
                    V.tensor_tensor(zv, sums[:, :, 0, :], zv, ALU.add).then_inc(z_rows, 1)

                def zt(half):
                    dve.wait_ge(zt_hi, 2 * blk_t + half + 1)
                    V.scalar_tensor_tensor(out=pad_z(1), in0=zt_bank[half][:, 0:HT].rearrange("p (r c) -> p r c", c=SEQ),
                                           scalar=0.0, in1=f32(pad_z(0)), op0=ALU.max, op1=ALU.subtract).then_inc(zt_lo, 1)

                def y_(half):
                    dve.wait_ge(y_psum, 2 * blk_t + half + 1)
                    dve.wait_ge(y_base, 2 * blk_t + half + 1)
                    V.tensor_tensor(y[:, half, :], y_bank[half][:, :], y[:, half, :], ALU.add).then_inc(y_rows, 1)

                def stat(half):
                    dve.wait_ge(y_rows, 2 * blk_t + half + 1)
                    for t in range(PAIRS):
                        last = V.bn_stats(stats[:, t, :], y[:, half, t * D:(t + 1) * D])
                    last.then_inc(y_stats, 1)

                def aggregate(half):
                    if not main:
                        dve.wait_ge(y_stats, 2 * blk_t + half + 1)
                    for t in range(PAIRS):
                        last = V.bn_aggr(mv[:, half, t, :], stats[:, t, :])
                    last.then_inc(y_moments, 1)

                def normalize(half):
                    dve.wait_ge(y_rstd, 2 * blk_t + half + 1)
                    for t in range(PAIRS):
                        v = y[:, half, t * D:(t + 1) * D]
                        last = V.tensor_scalar(v, v, mv[:, half, t, 0:1], rstd[:, half, t:t + 1],
                                               ALU.subtract, ALU.mult)
                    last.then_inc(y_norm, 1)

                if main:
                    h(0)
                if tail:
                    dve.wait_ge(t2_psum, blk_t + 1)
                    masked(t2f[:, :], t2_bank, 1, blk_t).then_inc(t2_masked, 1)
                    dve.wait_ge(t2_hi, blk_t + 1)
                    V.tensor_tensor(t2p[:, 1, :], t2f[:, :], f32(t2p[:, 0, :]), ALU.subtract).then_inc(t2_lo, 1)
                if main:
                    h(1)
                if tail:
                    dve.wait_ge(x2_psum, blk_t + 1)
                    for k in range(KD):
                        V.tensor_tensor(x1[:, 1 - par, k, :], x2_bank[k][:, :], x1[:, 1 - par, k, :],
                                        ALU.add).then_inc(x2_full, 1)
                    x2lo(0)
                if main:
                    h(2)
                if tail:
                    x3_(0)
                    x3t(0)
                if main:
                    h(3)
                if tail:
                    z_(0)
                    x2lo(1)
                    zt(0)
                if main:
                    h(4)
                if tail:
                    y_(0)
                    x3_(1)
                    stat(0)
                    x3t(1)
                    aggregate(0)
                if front:
                    if main:
                        dve.wait_ge(t1_lo, blk_f)
                    dve.wait_ge(t0_psum, blk_f + 1)
                    masked(tf[:, :], t0_bank, 0, blk_f).then_inc(t0_masked, 1)
                    if not main:
                        split_lo(1)
                        add_to(2)
                if main:
                    h(5)
                if front:
                    dve.wait_ge(t0_hi, blk_f + 1)
                    V.tensor_tensor(t0p[SEQ:P, :], tf[SEQ:P, :], f32(t0p[SEQ:P, :]), ALU.subtract).then_inc(t0_lo, 1)
                    if not main:
                        split_lo(2)
                        split_lo(3)
                if tail:
                    normalize(0)
                    z_(1)
                    zt(1)
                if main:
                    h(6)
                if front:
                    if tail:
                        dve.wait_ge(x2_lo, 2 * blk_t + 2)
                    dve.wait_ge(xe_ready, blk_f + 1)
                    for k in range(KD):
                        dve.wait_ge(x1_psum, 2 * blk_f + k + 1)
                        V.tensor_tensor(x1[:, 1 - par, k, :], x1_bank[k][:, :], x_in[:, k, :],
                                        ALU.add).then_inc(x1_full, 1)
                if tail:
                    y_(1)
                if front:
                    dve.wait_ge(x1_hi, blk_f + 1)
                    V.tensor_tensor(x1p[:, 1 - par, 1, :, :].rearrange("p k t -> p (k t)"),
                                    x1[:, 1 - par, :, :].rearrange("p k t -> p (k t)"),
                                    f32(x1p[:, 1 - par, 0, :, :]).rearrange("p k t -> p (k t)"),
                                    ALU.subtract).then_inc(x1_lo, 1)
                    if not main:
                        add_to(4)
                if tail:
                    stat(1)
                if main:
                    h(7)
                if tail:
                    aggregate(1)
                if front:
                    dve.wait_ge(t0_lo, blk_f + 1)
                    dve.wait_ge(t1_psum, blk_f + 1)
                    if not main:
                        split_lo(4)
                    masked(tf[:, :], t1_bank, 1, blk_f).then_inc(t1_masked, 1)
                if tail:
                    normalize(1)
                if front:
                    dve.wait_ge(t1_hi, blk_f + 1)
                    V.tensor_tensor(t1p[:, 1, :], tf[:, :], f32(t1p[:, 0, :]), ALU.subtract).then_inc(t1_lo, 1)
                    if first_block(n):
                        for c in LATE[7]:
                            split_lo(c)

            steps(dve, step)

        @block.gpsimd
        def _(pool):
            G = nc.gpsimd
            G.iota(group_i[:, 2:3], pattern=[[0, 1]], base=0, channel_multiplier=1).then_inc(consts_made, 1)
            G.memset(ident[:, :], 0.0).then_inc(ident_made, 1)
            pool.wait_ge(ident_made, 1)
            G.affine_select(out=ident[:, :], in_=ident[:, :], compare_op=ALU.not_equal, fill=1.0, base=0,
                            pattern=[[-1, P]], channel_multiplier=1).then_inc(ident_made, 1)
            pool.wait_ge(emb_made, 1)
            pool.wait_ge(consts_made, 2)

            def step(n, par, main, tail, front):
                blk_t, blk_f = n - 1, n + 1

                def base(half):
                    done = 2 * blk_t + half
                    pool.wait_ge(x3_rows, done + 1)
                    pool.wait_ge(adds_landed, 16 * HR * (done + 1))
                    pool.wait_ge(out_stored[half], 16 * blk_t)
                    x3v = x3[:, half, :].rearrange("p (t c) -> p t c", c=D)
                    G.tensor_tensor(y[:, half, :].rearrange("p (t c) -> p t c", c=D), x3v, adds[:, :, 0:D],
                                    ALU.add).then_inc(y_base, 1)
                    pool.wait_ge(x3t_psum, done + 1)
                    pool.wait_ge(y_base, done + 1)
                    G.tensor_tensor(x3v, x3v, adds[:, :, D:2 * D], ALU.add).then_inc(x3_base, 1)

                def inverse_deviation(half):
                    pool.wait_ge(y_moments, 2 * blk_t + half + 1)
                    G.tensor_tensor(rstd[:, half, :], mv[:, half, :, 1], eps[:, :], ALU.add).then_inc(var_eps, 1)
                    pool.wait_ge(var_eps, 2 * blk_t + half + 1)
                    G.tensor_tensor(rstd[:, half, :], rstd[:, half, :], minus_half[:, :], ALU.pow).then_inc(y_rstd, 1)

                def finish(half):
                    done = 2 * blk_t + half
                    pool.wait_ge(y_norm, done + 1)
                    pool.wait_ge(gains_landed, 16 * HR * (done + 1))
                    G.tensor_tensor(y[:, half, :], y[:, half, :], gains[:, :, :].rearrange("p t c -> p (t c)"),
                                    ALU.mult).then_inc(y_gained, 1)
                    pool.wait_ge(y_gained, done + 1)
                    pool.wait_ge(x3_base, done + 1)
                    G.tensor_tensor(y[:, half, :], y[:, half, :], x3[:, half, :], ALU.add).then_inc(out_rows, 1)

                if front:
                    pool.wait_ge(xh_ready, blk_f + 1)
                    G.tensor_tensor(x1p[:, 1 - par, 1, :, :].rearrange("p k t -> p (k t)"),
                                    x_in[:, :, :].rearrange("p k t -> p (k t)"),
                                    f32(x1p[:, 1 - par, 0, :, :]).rearrange("p k t -> p (k t)"),
                                    ALU.subtract).then_inc(xl_ready, 1)
                    pool.wait_ge(xl_ready, blk_f + 1)
                    for k in range(KD):
                        e = emb_cols[:, k, bass.ds(blk_f * BR, BR)].unsqueeze(2).broadcast_to([P, BR, SEQ])
                        v = x_in[:, k, :].rearrange("p (r c) -> p r c", c=SEQ)
                        last = G.tensor_tensor(v, v, e, ALU.add)
                    last.then_inc(xe_ready, 1)
                if tail:
                    base(0)
                    base(1)
                if tail:
                    inverse_deviation(0)
                    finish(0)
                    inverse_deviation(1)
                    finish(1)

            steps(pool, step)


def _layouts(i):
    import numpy as np
    c = np.ascontiguousarray
    tiles = lambda a: a.reshape(-1, P, a.shape[-1]).transpose(1, 0, 2).reshape(P, -1)
    la = i["L0_cond_lora_A"].reshape(LANGS * RANK, D).T
    la = np.concatenate([la, la], 1)
    lb = i["L0_cond_lora_B"].transpose(0, 2, 1).reshape(LANGS * RANK, D)
    lb = np.concatenate([lb, lb], 0)
    ewia = i["L1_cond_experts_wi_a"].reshape(EXPERTS * RANK, D).T
    ewib = i["L1_cond_experts_wi_b"].transpose(0, 2, 1).reshape(EXPERTS * RANK, F)
    ewoa = i["L1_cond_experts_wo_a"].reshape(EXPERTS * RANK, F).T
    ewob = i["L1_cond_experts_wo_b"].transpose(0, 2, 1).reshape(EXPERTS * RANK, D)
    sub = i["L2_cond_weight"].transpose(2, 0, 1).reshape(D, EXPERTS * D)
    down = i["L3_cond_down_w"].transpose(1, 0, 2).reshape(D, PROFILES * BOTTLE)
    up = i["L3_cond_up_w"].transpose(1, 0, 2).reshape(BOTTLE, PROFILES * D)
    wi, wo = i["L1_cond_wi"].T, tiles(i["L1_cond_wo"].T)
    w = np.concatenate([tiles(la), lb, tiles(ewia), ewob, ewib, tiles(wi[:, :512]), tiles(ewoa), wo[:, :CHUNK],
                        tiles(wi[:, 512:]), wo[:, CHUNK:], tiles(sub), tiles(down), up], 1)
    w = w.reshape(P, -1, CHUNK).transpose(1, 0, 2)
    return {
        "xT": c(i["x"].reshape(TOKENS, KD, P).transpose(2, 1, 0)),
        "lang": c(i["itok_B_0_3"].reshape(ROWS)), "expert": c(i["itok_B_0_7"].reshape(ROWS)),
        "profile": c(i["itok_B_0_6"].reshape(ROWS)),
        "lang_emb": c(i["L0_cond_lang_embed"]),
        "common_wi_a": c(i["L1_cond_common_wi_a"]), "common_wi_bT": c(i["L1_cond_common_wi_b"].T),
        "common_wo_a": c(i["L1_cond_common_wo_a"]), "common_wo_bT": c(i["L1_cond_common_wo_b"].T),
        "weights": c(w), "sub_b": c(i["L2_cond_bias"]),
        "prof_adds": c(np.concatenate([i["L3_cond_up_b"], i["L3_cond_ln_b"], i["L3_cond_down_b"]], 1)),
        "prof_g": c(i["L3_cond_ln_g"]),
    }


def kernel(**inputs):
    import numpy as np
    import concourse.bacc as bacc
    from concourse.bass_utils import run_bass_kernel_spmd

    arrays = _layouts({k: np.asarray(v) for k, v in inputs.items()})
    nc = bacc.Bacc("TRN2", target_bir_lowering=False, num_devices=1)
    args = [nc.dram_tensor(f"in_{k}", a.shape, mybir.dt.from_np(a.dtype), kind="ExternalInput").ap()
            for k, a in arrays.items()]
    out = nc.dram_tensor("out_rows", (TOKENS, D), F32, kind="ExternalOutput").ap()
    build(nc, *args, out)
    r = run_bass_kernel_spmd(nc, [{f"in_{k}": a for k, a in arrays.items()}], core_ids=[0])
    return r.results[0]["out_rows"].reshape(ROWS, SEQ, D)
```

```python
from contextlib import ExitStack

import concourse.bass as bass
from concourse import mybir

F32 = mybir.dt.float32
F32R = mybir.dt.float32r
I32 = mybir.dt.int32
ALU = mybir.AluOpType
ACT = mybir.ActivationFunctionType

P = 128
ROWS, SEQ, D = 128, 64, 256
TOKENS = ROWS * SEQ
KD = D // P
F = 1024
KF = F // P
RANK, LANGS, EXPERTS, PROFILES = 16, 4, 8, 8
BOTTLE = 128
ALPHA = 2.0
EPS = 1e-5
BR = 8
BT = BR * SEQ
BLOCKS = ROWS // BR
HR = BR // 2
HT = HR * SEQ
PAIRS = HR // 2
ADDS = 2 * D
CHUNK = 1024
CG = int(ALPHA) * RANK
LAST_LOADS = 16 * 3 * HR


def build(nc, xT, lang, expert, profile, lang_emb, common_small, common_wi_bT, common_wo_a,
          weights, sub_b, down_b, prof_adds, prof_g, out):
    ctx = ExitStack()
    with ctx:
        def sb(name, shape, dt=F32):
            return ctx.enter_context(nc.sbuf_tensor(name, shape, dt))

        def sem(name):
            return ctx.enter_context(nc.semaphore(name))

        w_small = sb("w_small", [P, 2, CHUNK], F32R)
        w_ewib = sb("w_ewib", [P, 2, F], F32R)
        w_wi = sb("w_wi", [P, 2, KD * F], F32R)
        w_ewoa = sb("w_ewoa", [P, 2, KF * P], F32R)
        w_wo = sb("w_wo", [P, 2, KF * D], F32R)
        w_sub = sb("w_sub", [P, 2, KD * EXPERTS * D], F32R)
        w_down = sb("w_down", [P, KD, PROFILES, 2, BOTTLE], F32R)
        w_up = sb("w_up", [P, 2, PROFILES * D], F32R)
        w_la = w_small[:, :, 0:2 * P].rearrange("p s (k m) -> p s k m", k=KD)
        w_lb = w_small[:, :, 256:512]
        w_ewia = w_small[:, :, 512:768].rearrange("p s (k m) -> p s k m", k=KD)
        w_ewob = w_small[:, :, 768:1024]

        ids = sb("ids", [1, 2 * ROWS], I32)
        group_i = sb("group_i", [P, 4], I32)
        group = sb("group", [P, 4])
        mask = sb("mask", [P, 2, ROWS])
        down_bias = sb("down_bias", [PROFILES, BOTTLE])
        row_cols = sb("row_cols", [P, KD + 1, ROWS])
        ident = sb("ident", [P, P])

        x_in = sb("x_in", [P, KD, BT])
        x1 = sb("x1", [P, 2, KD, BT])
        x1p = sb("x1p", [P, 2, 2, KD, BT], F32R)
        tf = sb("tf", [P, BT])
        t2f = sb("t2f", [P, BT])
        t0p = sb("t0p", [P, BT], F32R)
        t1p = sb("t1p", [P, 2, BT], F32R)
        t2p = sb("t2p", [P, 2, BT], F32R)
        hp = sb("hp", [P, 2, 2, BT], F32R)
        x2p = sb("x2p", [P, KD * PAIRS * 4 * SEQ], F32R)
        x3lo = sb("x3lo", [P, PAIRS * D])
        x3p = sb("x3p", [P, KD, HR, 2, SEQ], F32R)
        zpad = sb("zpad", [P, 2, HR * P], F32R)
        x3 = sb("x3", [P, 2, PAIRS * D])
        y = sb("y", [P, 2, PAIRS * D])
        sub_bias = sb("sub_bias", [P, PAIRS, D])
        adds = sb("adds", [P, PAIRS, ADDS])
        gains = sb("gains", [P, PAIRS, D])
        stats = sb("stats", [P, PAIRS, 6])
        mv = sb("mv", [P, 2, PAIRS, 2])
        rstd = sb("rstd", [P, 2, PAIRS])
        minus_half = sb("minus_half", [P, PAIRS])
        eps = sb("eps", [P, PAIRS])
        early = x1[:, 0, :, :].rearrange("p k t -> p (k t)")
        id_bc = early.bitcast(I32)[:, 0:3 * ROWS].rearrange("p (w r) -> p w r", w=3)
        id_f = early[:, 3 * ROWS:6 * ROWS].rearrange("p (w r) -> p w r", w=3)
        hot, hot_p = early[0:LANGS, 0:ROWS], early[0:PROFILES, ROWS:2 * ROWS]
        emb = early[0:LANGS, 6 * ROWS:6 * ROWS + D]
        stage = [t[:, :, :].rearrange("p s c -> p (s c)")[:, 0:CHUNK] for t in (y, x3, adds)]
        C = 3 * CG
        small_src, cb_i_src = t2f[0:C, 0:2 * D], x1[0:C, 1, :, :].rearrange("r k t -> r (k t)")
        ca_o_src = [t[0:C, :, :].rearrange("r t c -> r (t c)") for t in (gains, sub_bias)]
        small, cb_i = w_up[0:C, 0, 0:2 * D], w_up[0:C, 1, 0:F]
        ca_i, cb_o = small[:, 0:D], small[:, D:2 * D]
        ca_o = [w_up[0:C, 0, 1024:1536], w_up[0:C, 0, 1536:2048]]
        FACTORS = [(small_src, small, 2), (cb_i_src, cb_i, 1), (ca_o_src[0], ca_o[0], 1), (ca_o_src[1], ca_o[1], 1)]

        x3lo_own = [x3lo[:, :], x1[:, 1, 0, :]]
        x2p_own = [v.rearrange("p (k t b c) -> p k t b c", k=KD, t=PAIRS, b=4)
                   for v in (x2p[:, :], x1p[:, 0, 0, :, :].rearrange("p k t -> p (k t)"))]
        zpads = [zpad[:, :, :], t1p[:, :, :]]
        z_of_own = [t2f[:, :], tf[:, :]]
        zb_of_own = [v[:, 0:HT] for v in z_of_own]
        x3p_own = [x3p[:, :, :, :, :],
                   w_wi[:, 0, 0:KD * HR * P].rearrange("p (k r s c) -> p k r s c", k=KD, r=HR, s=2)]
        bias_of = [sub_bias[:, :, :], x_in[:, 0, :].rearrange("p (t c) -> p t c", c=D)]
        gains_of = [gains[:, :, :], x_in[:, 1, :].rearrange("p (t c) -> p t c", c=D)]
        bases_of = [adds[:, :, :], x1[:, 0, :, :]]

        banks = [ctx.enter_context(nc.psum_tensor(f"bank{i}", [P, 512], F32)) for i in range(8)]
        h_bank = banks[0:2]
        x2_bank = banks[2:4]
        t2_bank = banks[4]
        x3_bank, last_x3_bank = [(banks[5], banks[7]), (banks[7], banks[6])], [(banks[5], banks[7]), (banks[6], banks[4])]
        x3t_bank, last_x3t_bank = [banks[6], banks[5]], [banks[5], banks[6]]
        z_bank, last_z_bank = [(banks[7], banks[5]), (banks[7], banks[5])], [(banks[0], banks[1]), (banks[2], banks[3])]
        zt_bank, last_zt_bank = [banks[6], banks[6]], [banks[7], banks[4]]
        y_bank, last_y_bank = [banks[5], banks[6]], [banks[5], banks[6]]
        t0_bank = banks[6]
        x1_bank = [banks[5], banks[7]]
        t1_bank = banks[5]

        ids_landed = sem("ids_landed")
        tables_landed = sem("tables_landed")
        small_landed, common_b_landed, common_a_landed = sem("small_landed"), sem("common_b_landed"), sem("common_a_landed")
        stage_landed = [sem(f"stage{i}_landed") for i in range(len(stage))]
        chunk_split, chunk_split_g = sem("chunk_split"), sem("chunk_split_g")
        factor_hi, factor_split = sem("factor_hi"), sem("factor_split")
        consts_made = sem("consts_made")
        ident_made = sem("ident_made")
        setup_v = sem("setup_v")
        masks_made = sem("masks_made")
        emb_psum = sem("emb_psum")
        emb_made = sem("emb_made")
        common_psum = sem("common_psum")
        common_added = sem("common_added")
        chunk_hi = sem("chunk_hi")
        x_landed, xh_ready, xl_ready, xe_ready = sem("x_landed"), sem("xh_ready"), sem("xl_ready"), sem("xe_ready")
        t0_psum, t0_masked, t0_hi, t0_lo = sem("t0_psum"), sem("t0_masked"), sem("t0_hi"), sem("t0_lo")
        x1_psum, x1_full, x1_hi, x1_lo = sem("x1_psum"), sem("x1_full"), sem("x1_hi"), sem("x1_lo")
        t1_psum, t1_masked, t1_hi, t1_lo = sem("t1_psum"), sem("t1_masked"), sem("t1_hi"), sem("t1_lo")
        h_psum, h_hi, h_lo, h_used = sem("h_psum"), sem("h_hi"), sem("h_lo"), sem("h_used")
        t2_psum, t2_masked, t2_hi, t2_lo = sem("t2_psum"), sem("t2_masked"), sem("t2_hi"), sem("t2_lo")
        x2_psum, x2_full, x2_hi, x2_lo = sem("x2_psum"), sem("x2_full"), sem("x2_hi"), sem("x2_lo")
        x3_psum, x3_moved, x3_biased, x3_rows = sem("x3_psum"), sem("x3_moved"), sem("x3_biased"), sem("x3_rows")
        x3t_psum, x3t_hi, x3t_lo = sem("x3t_psum"), sem("x3t_hi"), sem("x3t_lo")
        z_psum, z_lo, z_rows = sem("z_psum"), sem("z_lo"), sem("z_rows")
        zt_psum, zt_lo_sum, zt_biased, zt_hi, zt_lo = sem("zt_psum"), sem("zt_lo_sum"), sem("zt_biased"), sem("zt_hi"), sem("zt_lo")
        y_base, x3_base = sem("y_base"), sem("x3_base")
        y_psum, y_rows, y_stats, y_moments = sem("y_psum"), sem("y_rows"), sem("y_stats"), sem("y_moments")
        var_eps, y_rstd, y_norm, y_gained, out_rows = sem("var_eps"), sem("y_rstd"), sem("y_norm"), sem("y_gained"), sem("out_rows")
        bias_landed, adds_landed, gains_landed = sem("bias_landed"), sem("adds_landed"), sem("gains_landed")
        pads_cleared, last_landed = sem("pads_cleared"), sem("last_landed")
        last_gained, last_rows = sem("last_gained"), sem("last_rows")
        out_stored = [sem("out0_stored"), sem("out1_stored")]

        block = ctx.enter_context(nc.Block())

        N_CHUNKS = weights.shape[0]

        def columns(t, c):
            return lambda part: t[:, part, c * CHUNK:(c + 1) * CHUNK]

        def wi_columns(j):
            return lambda part: w_wi[:, part, :].rearrange("p (k f) -> p k f", k=KD)[:, :, j * 512:(j + 1) * 512]

        def down_columns(k):
            return lambda part: w_down[:, k, :, part, :]

        CHUNKS = [columns(w_small, 0), columns(w_ewib, 0), wi_columns(0), columns(w_ewoa, 0), columns(w_wo, 0),
                  wi_columns(1), columns(w_wo, 1), *(columns(w_sub, c) for c in range(4)), down_columns(0),
                  down_columns(1), columns(w_up, 0), columns(w_up, 1)]
        assert len(CHUNKS) == N_CHUNKS
        WI_CHUNKS, WO_CHUNKS, SUB_CHUNKS, DOWN_CHUNKS = (2, 5), (4, 6), (7, 8, 9, 10), (11, 12)
        SPLIT_G = (1, 3, 11, 12, 13, 14)
        SPLIT_V = tuple(c for c in range(N_CHUNKS) if c not in SPLIT_G)
        ADDED = (2, 4, 5, 6, 7, 8, 9, 10)
        COMMON_BANKS = {2: (0, 1), 4: (2, 3), 5: (4, 6), 6: (5, 7)}
        LATE_HI = [(4, 5), (6,), (7,), (8,), (9,), (10, 11), (12,), (13, 14)]
        LATE_LO = [(4,), (5,), (6,), (7,), (8,), (9, 10), (), ()]
        LATE_ADD = [(6,), (7,), (8,), (9,), (10,), (), (), ()]

        def staged(c):
            v = stage[c % len(stage)]
            if c in WI_CHUNKS:
                return v.rearrange("p (k f) -> p k f", k=KD)
            return v.rearrange("p (e k) -> p e k", k=BOTTLE) if c in DOWN_CHUNKS else v

        def wait_staged(eng, c):
            eng.wait_ge(stage_landed[c % len(stage)], 16 * (c // len(stage) + 1))

        def wait_chunk(eng, c):
            if c in SPLIT_G:
                eng.wait_ge(chunk_split_g, 1 + SPLIT_G.index(c))
            else:
                eng.wait_ge(chunk_split, 1 + SPLIT_V.index(c))

        def wait_split(eng):
            wait_chunk(eng, SPLIT_V[-1])
            wait_chunk(eng, SPLIT_G[-1])

        def f32(ap):
            return ap.bitcast(F32)

        def rows_of(v):
            return v.rearrange("p k (r c) -> p k r c", c=SEQ)

        def x2_part(part, own, k):
            return x2p_own[own][:, k, :, 1:3, :] if part else x2p_own[own][:, k, :, 0:4:3, :]

        def half_tokens(par, k, half):
            return x1[:, par, k, half * HT:(half + 1) * HT].rearrange("p (t r c) -> p t r c", r=2, c=SEQ)

        def pad_z(part, own):
            return zpads[own][:, part, :].rearrange("p (r c) -> p r c", c=P)[:, :, 0:SEQ]

        def z_parts(t, own, two):
            return (z_of_own[own][:, t * 2 * BOTTLE:(t + 1) * 2 * BOTTLE].rearrange("p (r c) -> p r c", c=BOTTLE),
                    two[t][:, :].rearrange("p (r s c) -> p r s c", s=2, c=BOTTLE))

        def row_ids(engine, base, row0):
            _, values = nc.values_load_multi_w_load_instructions(
                ids[0:1, bass.ds(base + row0, HR)], engines=(engine,), min_val=0, max_val=EXPERTS - 1,
                skip_runtime_bounds_check_because="an id names one of the tables' EXPERTS or PROFILES entries")
            return values

        def first_block(n):
            return isinstance(n, int) and n == 0

        def steps(eng, step, last_tail):
            step(-1, 1, False, False, True)
            step(0, 0, True, False, True)
            step(1, 1, True, True, True)
            with eng.Fori(1, BLOCKS // 2 - 1) as i:
                step(2 * i, 0, True, True, True)
                step(2 * i + 1, 1, True, True, True)
            step(BLOCKS - 2, 0, True, True, True)
            step(BLOCKS - 1, 1, True, True, False)
            last_tail(BLOCKS - 1, 1)

        @block.sync
        def _(sp):
            def load_chunk(c):
                if c >= len(stage):
                    wait_chunk(sp, c - len(stage))
                sp.dma_start(stage[c % len(stage)], weights[c]).then_inc(stage_landed[c % len(stage)], 16)

            def load_x(blk):
                sp.dma_start(x_in[:, :, :], xT[:, :, bass.ds(blk * BT, BT)]).then_inc(x_landed, 16)

            def load_rows(dst, src, rows, landed):
                for r in range(HR):
                    q = slice((r % 2) * SEQ, (r % 2) * SEQ + SEQ)
                    row = src[bass.ds(rows[r], 1), :].rearrange("a c -> (a c)")
                    sp.dma_start(dst[q, r // 2, :], row.partition_broadcast(SEQ)).then_inc(landed, 16)

            def load_tables(blk, half):
                done = 2 * blk + half
                row0 = blk * BR + half * HR
                es = row_ids(mybir.EngineType.SP, 0, row0)
                sp.wait_ge(x3_rows, done)
                load_rows(bias_of[0], sub_b, es, bias_landed)
                ps = row_ids(mybir.EngineType.SP, ROWS, row0)
                if first_block(blk) and half == 0:
                    wait_split(sp)
                sp.wait_ge(x3_base, done)
                load_rows(adds, prof_adds, ps, adds_landed)
                sp.wait_ge(y_gained, done)
                load_rows(gains_of[0], prof_g, ps, gains_landed)

            def load_last_bias_gains():
                sp.wait_ge(x1_full, 2 * BLOCKS)
                load_rows(bias_of[1], sub_b, row_ids(mybir.EngineType.SP, 0, ROWS - HR), last_landed)
                load_rows(gains_of[1], prof_g, row_ids(mybir.EngineType.SP, ROWS, ROWS - HR), last_landed)

            def load_last_bases():
                sp.wait_ge(x2_lo, 2 * BLOCKS - 2)
                load_rows(bases_of[1], prof_adds, row_ids(mybir.EngineType.SP, ROWS, ROWS - HR), last_landed)

            def store(blk, half, rows_done=True):
                if rows_done:
                    sp.wait_ge(out_rows, 2 * blk + half + 1)
                dst = out[bass.ds(blk * BT + half * HT, HT), :].rearrange("(t p) c -> p t c", p=P)
                sp.dma_start(dst, y[:, half, :].rearrange("p (t c) -> p t c", c=D)).then_inc(out_stored[half], 16)

            def step(n, par, main, tail, front):
                blk_t, blk_f = n - 1, n + 1
                if not main:
                    load_chunk(0)
                    load_x(blk_f)
                    sp.dma_start(id_bc[:, 0, :], lang.partition_broadcast(P)).then_inc(tables_landed, 16)
                    sp.dma_start(id_bc[:, 1, :], expert.partition_broadcast(P)).then_inc(tables_landed, 16)
                    sp.dma_start(id_bc[:, 2, :], profile.partition_broadcast(P)).then_inc(tables_landed, 16)
                    sp.dma_start(emb[:, :], lang_emb).then_inc(tables_landed, 16)
                    sp.dma_start(down_bias[:, :], down_b).then_inc(tables_landed, 16)
                    sp.dma_start(small_src, common_small).then_inc(small_landed, 16)
                    sp.dma_start(cb_i_src, common_wi_bT).then_inc(common_b_landed, 16)
                    load_chunk(1)
                    load_chunk(2)
                    for j in range(2):
                        sp.dma_start(ca_o_src[j], common_wo_a[:, j * 512:(j + 1) * 512]).then_inc(common_a_landed, 16)
                    sp.dma_start(ids[0:1, 0:ROWS], expert).then_inc(ids_landed, 16)
                    sp.dma_start(ids[0:1, ROWS:2 * ROWS], profile).then_inc(ids_landed, 16)
                    for c in range(3, 6):
                        load_chunk(c)
                    sp.wait_ge(ids_landed, 32)
                elif front:
                    sp.wait_ge(x1_full, 2 * blk_f)
                    load_x(blk_f)
                if first_block(n):
                    for c in range(6, N_CHUNKS):
                        load_chunk(c)
                if tail:
                    load_tables(blk_t, 0)
                    if not front:
                        load_last_bias_gains()
                    load_tables(blk_t, 1)
                    if not front:
                        load_last_bases()
                    store(blk_t, 0)
                    if front:
                        store(blk_t, 1)

            def last_tail(blk, par):
                load_tables(blk, 0)
                store(blk - 1, 1)
                store(blk, 0)
                sp.wait_ge(last_rows, 1)
                store(blk, 1, rows_done=False)

            steps(sp, step, last_tail)
            sp.wait_ge(out_stored[0], 16 * BLOCKS)
            sp.wait_ge(out_stored[1], 16 * BLOCKS)

        @block.tensor
        def _(pe):
            def mm_hi(bank, w, x, first):
                nc.tensor.matmul(bank, w(0), x(0), start=first, stop=False)
                nc.tensor.matmul(bank, w(1), x(0), start=False, stop=False)

            def mm_lo(bank, w, x, last):
                return nc.tensor.matmul(bank, w(0), x(1), start=False, stop=last)

            def mm3(bank, w, x, first, last):
                mm_hi(bank, w, x, first)
                return mm_lo(bank, w, x, last)

            def embeddings():
                pe.wait_ge(masks_made, 1)
                nc.tensor.matmul(t2_bank[:, KD * ROWS:(KD + 1) * ROWS], down_bias[:, :], hot_p[:, :], start=True, stop=True)
                for k in range(KD):
                    last = nc.tensor.matmul(t2_bank[:, k * ROWS:(k + 1) * ROWS], emb[:, k * P:(k + 1) * P], hot[:, :],
                                            start=True, stop=True)
                last.then_inc(emb_psum, 1)

            def common(c):
                two = [banks[b] for b in COMMON_BANKS[c]]
                if c in WI_CHUNKS:
                    f = WI_CHUNKS.index(c) * 512
                    for k in range(KD):
                        last = nc.tensor.matmul(two[k][:, :], ca_i[:, k * P:(k + 1) * P], cb_i[:, f:f + 512],
                                                start=True, stop=True)
                else:
                    for q in range(4):
                        last = nc.tensor.matmul(two[q // 2][:, (q % 2) * D:(q % 2) * D + D],
                                                ca_o[WO_CHUNKS.index(c)][:, q * P:(q + 1) * P], cb_o,
                                                start=True, stop=True)
                last.then_inc(common_psum, 1)

            pe.wait_ge(ident_made, 2)
            pe.wait_ge(consts_made, 2)

            def w_of(t, lo, n=P):
                return lambda part: t[:, part, lo:lo + n]

            def hidden(n, par, m):
                if m >= 2 or not first_block(n):
                    pe.wait_ge(h_lo, 8 * n + m - 1)
                bank = h_bank[m % 2][:, :]
                if first_block(n) and m in (0, 4):
                    wait_chunk(pe, WI_CHUNKS[m // 4])
                for k in range(KD):
                    mm3(bank, w_of(w_wi, k * F + m * P), lambda part: x1p[:, par, part, k, :], k == 0, False)
                t1_of = lambda part: t1p[:, part, :]
                if m == 0:
                    if first_block(n):
                        wait_chunk(pe, 1)
                    pe.wait_ge(t1_hi, n + 1)
                mm_hi(bank, w_of(w_ewib, m * P), t1_of, False)
                if m == 0:
                    pe.wait_ge(t1_lo, n + 1)
                mm_lo(bank, w_of(w_ewib, m * P), t1_of, True).then_inc(h_psum, 1)

            def outputs(n, m):
                if first_block(n) and m in (0, 4):
                    wait_chunk(pe, WO_CHUNKS[m // 4])
                    wait_chunk(pe, 3)
                if m == 0:
                    pe.wait_ge(x2_full, 2 * n)
                    pe.wait_ge(t2_masked, n)
                pe.wait_ge(h_hi, 8 * n + m + 1)
                pe.wait_ge(h_lo, 8 * n + m + 1)
                hid = lambda part: hp[:, m % 2, part, :]
                last = mm3(t2_bank[:, :], w_of(w_ewoa, m * P), hid, m == 0, m == KF - 1)
                if m == KF - 1:
                    last.then_inc(t2_psum, 1)
                for k in range(KD):
                    last = mm3(x2_bank[k][:, :], w_of(w_wo, m * D + k * P), hid, m == 0, False)
                last.then_inc(h_used, 1)

            def t0(blk, par):
                if first_block(blk):
                    wait_chunk(pe, 0)
                pe.wait_ge(xh_ready, blk + 1)
                pe.wait_ge(xl_ready, blk + 1)
                for k in range(KD):
                    last = mm3(t0_bank[:, :], lambda part: w_la[:, part, k, :],
                               lambda part: x1p[:, par, part, k, :], k == 0, k == KD - 1)
                last.then_inc(t0_psum, 1)

            def x1_cols(blk):
                pe.wait_ge(t0_hi, blk + 1)
                pe.wait_ge(t0_lo, blk + 1)
                for k in range(KD):
                    for part in range(2):
                        last = nc.tensor.matmul(x1_bank[k][:, :], w_lb[:, part, k * P:(k + 1) * P], t0p[:, :],
                                                start=part == 0, stop=part == 1)
                    last.then_inc(x1_psum, 1)

            def t1(blk, par):
                pe.wait_ge(x1_full, 2 * blk + 2)
                pe.wait_ge(x1_hi, blk + 1)
                for k in range(KD):
                    mm_hi(t1_bank[:, :], lambda part: w_ewia[:, part, k, :], lambda part: x1p[:, par, part, k, :], k == 0)
                pe.wait_ge(x1_lo, blk + 1)
                for k in range(KD):
                    last = mm_lo(t1_bank[:, :], lambda part: w_ewia[:, part, k, :],
                                 lambda part: x1p[:, par, part, k, :], k == KD - 1)
                last.then_inc(t1_psum, 1)

            def x2_cols(blk):
                pe.wait_ge(t2_hi, blk + 1)
                for k in range(KD):
                    mm_hi(x2_bank[k][:, :], w_of(w_ewob, k * P), lambda part: t2p[:, part, :], False)
                pe.wait_ge(t2_lo, blk + 1)
                for k in range(KD):
                    last = mm_lo(x2_bank[k][:, :], w_of(w_ewob, k * P), lambda part: t2p[:, part, :], True)
                last.then_inc(x2_psum, 1)

            def mm_hi_rows(bank, x, w, first):
                nc.tensor.matmul(bank, x(0), w(0), start=first, stop=False)
                nc.tensor.matmul(bank, x(0), w(1), start=False, stop=False)

            def mm_lo_rows(bank, x, w, last):
                return nc.tensor.matmul(bank, x(1), w(0), start=False, stop=last)

            def window(t, r):
                lo = r * P - (r % 2) * SEQ
                return lambda part: t(part)[:, lo:lo + P]

            def experts_of(blk, half):
                return row_ids(mybir.EngineType.PE, 0, blk * BR + half * HR)

            def x3_of(blk, half, es, own=0, bank_of=x3_bank):
                pe.wait_ge(x2_hi, 2 * blk + half + 1)
                pe.wait_ge(x2_lo, 2 * blk + half + 1)
                for r in range(HR):
                    t, odd = r // 2, r % 2
                    for k in range(KD):
                        both = x2p_own[own][:, k, t, 2 * odd:2 * odd + 2, :].rearrange("p b c -> p (b c)")
                        for part in range(2):
                            last = nc.tensor.matmul(
                                bank_of[half][odd][:, t * D:(t + 1) * D], both,
                                w_sub[:, part, bass.ds(es[r] * D + k * EXPERTS * D, D)],
                                start=k == 0 and part == 0, stop=k == KD - 1 and part == 1)
                last.then_inc(x3_psum, 1)

            def x3t(blk, half, bank_of=x3t_bank):
                pe.wait_ge(x3_rows, 2 * blk + half + 1)
                for k in range(KD):
                    for t in range(PAIRS):
                        last = nc.tensor.transpose(bank_of[half][:, k * HT + t * P:k * HT + (t + 1) * P],
                                                   x3[:, half, t * D + k * P:t * D + (k + 1) * P], ident[:, :])
                last.then_inc(x3t_psum, 1)

            def z_of(blk, half, own=0, bank_of=z_bank):
                ps = row_ids(mybir.EngineType.PE, ROWS, blk * BR + half * HR)
                pe.wait_ge(x3t_hi, 2 * blk + half + 1)
                pe.wait_ge(x3t_lo, 2 * blk + half + 1)
                for r in range(HR):
                    bank = bank_of[half][r // 2][:, (r % 2) * 2 * BOTTLE:(r % 2 + 1) * 2 * BOTTLE]
                    for k in range(KD):
                        both = w_down[:, k, :, :, :].rearrange("p e s k -> p (e s k)")[
                            :, bass.ds(ps[r] * 2 * BOTTLE, 2 * BOTTLE)]
                        last = nc.tensor.matmul(bank, x3p_own[own][:, k, r, :, :].rearrange("p s c -> p (s c)"), both,
                                                start=k == 0, stop=k == KD - 1)
                last.then_inc(z_psum, 1)
                return ps

            def zt(blk, half, own=0, bank_of=zt_bank):
                pe.wait_ge(z_rows, 2 * blk + half + 1)
                for r in range(HR):
                    last = nc.tensor.transpose(bank_of[half][:, r * P:(r + 1) * P],
                                               z_of_own[own][:, r * BOTTLE:(r + 1) * BOTTLE], ident[:, :])
                last.then_inc(zt_psum, 1)

            def y_of(blk, half, ps, own=0, bank_of=y_bank):
                def operands(r):
                    return (bank_of[half][:, (r // 2) * D:(r // 2) * D + D],
                            window(lambda part: zpads[own][:, part, :], r),
                            lambda part: w_up[:, part, bass.ds(ps[r] * D, D)])

                pe.wait_ge(zt_hi, 2 * blk + half + 1)
                for t in range(PAIRS):
                    for r in (2 * t, 2 * t + 1):
                        mm_hi_rows(*operands(r), r % 2 == 0)
                    if t == 0:
                        pe.wait_ge(zt_lo, 2 * blk + half + 1)
                    for r in (2 * t, 2 * t + 1):
                        last = mm_lo_rows(*operands(r), r % 2 == 1)
                last.then_inc(y_psum, 1)

            def first_front():
                t0(0, 0)
                embeddings()
                pe.wait_ge(factor_split, 2)
                common(2)
                x1_cols(0)
                pe.wait_ge(emb_made, 1)
                common(5)
                t1(0, 0)
                pe.wait_ge(factor_split, 3)
                common(4)
                pe.wait_ge(ids_landed, 32)

            def step(n, par, main, tail, front):
                blk_t, blk_f = n - 1, n + 1
                if not main:
                    first_front()
                    return
                hidden(n, par, 0)
                if first_block(n):
                    pe.wait_ge(factor_split, 4)
                    common(6)
                if tail:
                    outputs(blk_t, KF - 1)
                hidden(n, par, 1)
                if tail:
                    x2_cols(blk_t)
                hidden(n, par, 2)
                if first_block(n):
                    pe.wait_ge(common_added, 3)
                outputs(n, 0)
                if tail:
                    if first_block(blk_t):
                        wait_split(pe)
                    pe.wait_ge(x1_full, 2 * n + 2)
                    pe.wait_ge(t1_masked, n + 1)
                    x3_of(blk_t, 0, experts_of(blk_t, 0))
                outputs(n, 1)
                hidden(n, par, 3)
                if tail:
                    pe.wait_ge(y_rows, 2 * blk_t)
                    x3t(blk_t, 0)
                outputs(n, 2)
                if tail:
                    ps = z_of(blk_t, 0)
                hidden(n, par, 4)
                if tail:
                    es = experts_of(blk_t, 1)
                    zt(blk_t, 0)
                outputs(n, 3)
                if tail:
                    y_of(blk_t, 0, ps)
                    x3_of(blk_t, 1, es)
                hidden(n, par, 5)
                outputs(n, 4)
                if tail:
                    pe.wait_ge(y_rows, 2 * blk_t + 1)
                    x3t(blk_t, 1)
                if front:
                    t0(blk_f, 1 - par)
                hidden(n, par, 6)
                if tail:
                    ps = z_of(blk_t, 1)
                outputs(n, 5)
                if tail:
                    if front:
                        pe.wait_ge(t0_masked, blk_f + 1)
                    zt(blk_t, 1)
                if front:
                    x1_cols(blk_f)
                hidden(n, par, 7)
                if tail:
                    y_of(blk_t, 1, ps)
                if front:
                    t1(blk_f, 1 - par)
                    outputs(n, 6)

            def last_outputs(blk):
                def hid(m):
                    return lambda part: hp[:, m % 2, part, :]

                def t2_over(m):
                    return mm3(t2_bank[:, :], w_of(w_ewoa, m * P), hid(m), False, m == KF - 1)

                def x2_over(m, k):
                    mm3(x2_bank[k][:, :], w_of(w_wo, m * D + k * P), hid(m), False, False)

                m = KF - 2
                pe.wait_ge(h_hi, 8 * blk + m + 1)
                pe.wait_ge(h_lo, 8 * blk + m + 1)
                t2_over(m)
                x2_over(m, 0)
                pe.wait_ge(h_hi, 8 * blk + m + 2)
                pe.wait_ge(h_lo, 8 * blk + m + 2)
                t2_over(m + 1).then_inc(t2_psum, 1)
                x2_over(m, 1)
                x2_over(m + 1, 0)
                x2_over(m + 1, 1)
                pe.wait_ge(t2_hi, blk + 1)
                pe.wait_ge(t2_lo, blk + 1)
                for k in range(KD):
                    mm3(x2_bank[k][:, :], w_of(w_ewob, k * P), lambda part: t2p[:, part, :], False, True).then_inc(x2_psum, 1)

            def last_tail(blk, par):
                last_outputs(blk)
                pe.wait_ge(y_rows, 2 * blk)
                for half in range(2):
                    x3_of(blk, half, experts_of(blk, half), half, last_x3_bank)
                for half in range(2):
                    x3t(blk, half, last_x3t_bank)
                ps = [z_of(blk, half, half, last_z_bank) for half in range(2)]
                for half in range(2):
                    zt(blk, half, half, last_zt_bank)
                for half in range(2):
                    y_of(blk, half, ps[half], half, last_y_bank)

            steps(pe, step, last_tail)

        @block.scalar
        def _(act):
            def copy(dst, src, scale=1.0):
                return nc.scalar.activation(dst, src, ACT.Copy, scale=scale)

            def split_hi(c):
                if c in ADDED:
                    act.wait_ge(common_added, 1 + ADDED.index(c))
                else:
                    wait_staged(act, c)
                copy(CHUNKS[c](0), staged(c)).then_inc(chunk_hi, 1)

            def late(m):
                for c in LATE_HI[m]:
                    split_hi(c)

            def h(n, m):
                if m >= 2 or not first_block(n):
                    act.wait_ge(h_used, 8 * n + m - 1)
                act.wait_ge(h_psum, 8 * n + m + 1)
                nc.scalar.activation(hp[:, m % 2, 0, :], h_bank[m % 2][:, :], ACT.Relu).then_inc(h_hi, 1)
                if first_block(n) and m < 4:
                    late(m)

            def t2(blk):
                act.wait_ge(x2_psum, blk)
                act.wait_ge(t2_masked, blk + 1)
                copy(t2p[:, 0, :], t2f[:, :]).then_inc(t2_hi, 1)

            def x2(blk, par, half, own=0):
                if not own:
                    act.wait_ge(x3_psum, 2 * blk + half)
                act.wait_ge(x2_full, 2 * blk + 2)
                for k in range(KD):
                    last = copy(x2_part(0, own, k), half_tokens(par, k, half))
                last.then_inc(x2_hi, 1)

            def x3_lo(blk, half, own=0, bank_of=x3_bank):
                if own:
                    act.wait_ge(x2_lo, 2 * BLOCKS)
                else:
                    act.wait_ge(x3_rows, 2 * blk + half)
                act.wait_ge(x3_psum, 2 * blk + half + 1)
                even, odd = bank_of[half]
                copy(x3lo_own[own][0:SEQ], even[SEQ:P, :])
                copy(x3lo_own[own][SEQ:P], odd[0:SEQ, :]).then_inc(x3_moved, 1)

            def x3t(blk, half, own=0, bank_of=x3t_bank):
                if not own:
                    act.wait_ge(z_psum, 2 * blk + half)
                act.wait_ge(x3t_psum, 2 * blk + half + 1)
                copy(x3p_own[own][:, :, :, 0, :],
                     rows_of(bank_of[half][:, :].rearrange("p (k t) -> p k t", k=KD))).then_inc(x3t_hi, 1)

            def z_(blk, half, own=0, bank_of=z_bank):
                if own:
                    act.wait_ge(t1_lo, BLOCKS)
                else:
                    act.wait_ge(t2_lo, blk + 1)
                    act.wait_ge(zt_lo, 2 * blk + half)
                act.wait_ge(z_psum, 2 * blk + half + 1)
                for t in range(PAIRS):
                    v, sums = z_parts(t, own, bank_of[half])
                    last = copy(v, sums[:, :, 1, :])
                last.then_inc(z_lo, 1)

            def zt(blk, half, own=0):
                if own:
                    act.wait_ge(pads_cleared, 1)
                else:
                    act.wait_ge(y_psum, 2 * blk + half)
                act.wait_ge(zt_biased, 2 * blk + half + 1)
                nc.scalar.activation(pad_z(0, own), zb_of_own[own].rearrange("p (r c) -> p r c", c=SEQ),
                                     ACT.Relu).then_inc(zt_hi, 1)

            def x_hi(blk, par):
                act.wait_ge(x_landed, 16 * blk + 16)
                copy(x1p[:, par, 0, :, :].rearrange("p k t -> p (k t)"),
                     x_in[:, :, :].rearrange("p k t -> p (k t)")).then_inc(xh_ready, 1)

            def t0(blk):
                act.wait_ge(t0_masked, blk + 1)
                copy(t0p[:, :], tf[:, :]).then_inc(t0_hi, 1)

            def x1_hi_of(blk, par):
                act.wait_ge(x1_full, 2 * blk + 2)
                copy(x1p[:, par, 0, :, :].rearrange("p k t -> p (k t)"),
                     x1[:, par, :, :].rearrange("p k t -> p (k t)")).then_inc(x1_hi, 1)

            def t1(blk):
                act.wait_ge(t1_masked, blk + 1)
                copy(t1p[:, 0, :], tf[:, :]).then_inc(t1_hi, 1)

            def factor(j, landed, count):
                act.wait_ge(landed, count)
                copy(FACTORS[j][1], FACTORS[j][0]).then_inc(factor_hi, 1)

            def first_front():
                split_hi(0)
                x_hi(0, 0)
                factor(0, small_landed, 16)
                factor(1, common_b_landed, 16)
                split_hi(1)
                t0(0)
                act.wait_ge(emb_psum, 1)
                copy(row_cols[:, :, :].rearrange("p k r -> p (k r)"), t2_bank[:, 0:(KD + 1) * ROWS]).then_inc(emb_made, 1)
                factor(2, common_a_landed, 32)
                split_hi(2)
                x1_hi_of(0, 0)
                split_hi(3)
                factor(3, common_a_landed, 32)
                t1(0)

            def step(n, par, main, tail, front):
                blk_t, blk_f = n - 1, n + 1
                if not main:
                    first_front()
                    return
                h(n, 0)
                if tail:
                    t2(blk_t)
                h(n, 1)
                if tail:
                    x2(blk_t, 1 - par, 0)
                if front:
                    act.wait_ge(h_psum, 8 * n)
                    x_hi(blk_f, 1 - par)
                h(n, 2)
                if tail:
                    x3_lo(blk_t, 0)
                h(n, 3)
                if tail:
                    x3t(blk_t, 0)
                    x2(blk_t, 1 - par, 1)
                    z_(blk_t, 0)
                h(n, 4)
                if first_block(n):
                    late(4)
                if tail:
                    zt(blk_t, 0)
                    x3_lo(blk_t, 1)
                h(n, 5)
                if first_block(n):
                    late(5)
                if tail:
                    x3t(blk_t, 1)
                if front:
                    act.wait_ge(x1_psum, 2 * blk_f)
                    t0(blk_f)
                h(n, 6)
                if tail:
                    z_(blk_t, 1)
                    zt(blk_t, 1)
                if front:
                    x1_hi_of(blk_f, 1 - par)
                if first_block(n):
                    late(6)
                h(n, 7)
                if front:
                    act.wait_ge(h_psum, 8 * n + 8)
                    t1(blk_f)
                if first_block(n):
                    late(7)

            def last_tail(blk, par):
                t2(blk)
                for half in range(2):
                    x2(blk, par, half, half)
                for half in range(2):
                    x3_lo(blk, half, half, last_x3_bank)
                for half in range(2):
                    x3t(blk, half, half, last_x3t_bank)
                for half in range(2):
                    z_(blk, half, half, last_z_bank)
                for half in range(2):
                    zt(blk, half, half)

            steps(act, step, last_tail)

        @block.vector
        def _(dve):
            V = nc.vector
            dve.wait_ge(consts_made, 1)
            V.tensor_scalar(group_i[:, 1:2], group_i[:, 2:3], 4, None, ALU.arith_shift_right).then_inc(setup_v, 1)
            dve.wait_ge(setup_v, 1)
            V.tensor_scalar(group_i[:, 0:1], group_i[:, 1:2], 3, None, ALU.bitwise_and).then_inc(setup_v, 1)
            dve.wait_ge(setup_v, 2)
            V.tensor_copy(group[:, 0:3], group_i[:, 0:3]).then_inc(setup_v, 1)

            def make_masks():
                dve.wait_ge(tables_landed, 80)
                V.tensor_copy(id_f, id_bc).then_inc(setup_v, 1)
                dve.wait_ge(setup_v, 4)
                V.tensor_scalar(mask[:, 0, :], id_f[:, 0, :], group[:, 0:1], None, ALU.is_equal)
                V.tensor_scalar(mask[:, 1, :], id_f[:, 1, :], group[:, 1:2], ALPHA, ALU.is_equal, ALU.mult)
                V.tensor_scalar(hot_p[:, :], id_f[0:PROFILES, 2, :], group[0:PROFILES, 2:3], None, ALU.is_equal)
                V.tensor_scalar(hot[:, :], id_f[0:LANGS, 0, :], group[0:LANGS, 2:3], None,
                                ALU.is_equal).then_inc(masks_made, 1)

            def add_to(c):
                wait_staged(dve, c)
                src = stage[c % len(stage)]
                if c in SUB_CHUNKS:
                    dve.wait_ge(ident_made, 2)
                    k = (c - SUB_CHUNKS[0]) // 2
                    diag = src.rearrange("p (e o) -> p e o", o=D)[:, :, k * P:(k + 1) * P]
                    last = V.tensor_tensor(diag, diag, ident[:, :].unsqueeze(1).broadcast_to([P, 4, P]), ALU.add)
                else:
                    dve.wait_ge(common_psum, 1 + (2, 5, 4, 6).index(c))
                    for j, bank in enumerate(COMMON_BANKS[c]):
                        v = src[:, j * 512:(j + 1) * 512]
                        last = V.tensor_tensor(v, banks[bank][:, :], v, ALU.add)
                last.then_inc(common_added, 1)

            def split_lo(c):
                dve.wait_ge(chunk_hi, c + 1)
                dst = CHUNKS[c]
                V.tensor_tensor(dst(1), staged(c), f32(dst(0)), ALU.subtract).then_inc(chunk_split, 1)

            def late(m):
                for c in LATE_LO[m]:
                    split_lo(c)
                for c in LATE_ADD[m]:
                    add_to(c)

            def h(n, m):
                dve.wait_ge(h_hi, 8 * n + m + 1)
                V.scalar_tensor_tensor(out=hp[:, m % 2, 1, :], in0=h_bank[m % 2][:, :], scalar=0.0,
                                       in1=f32(hp[:, m % 2, 0, :]), op0=ALU.max, op1=ALU.subtract).then_inc(h_lo, 1)
                if first_block(n) and m < 4:
                    late(m)

            def masked(dst, bank, which, blk):
                m = mask[:, which, bass.ds(blk * BR, BR)].unsqueeze(2).broadcast_to([P, BR, SEQ])
                return V.tensor_tensor(dst.rearrange("p (r c) -> p r c", c=SEQ),
                                       bank[:, :].rearrange("p (r c) -> p r c", c=SEQ), m, ALU.mult)

            def t2(blk):
                dve.wait_ge(t2_psum, blk + 1)
                masked(t2f[:, :], t2_bank, 1, blk).then_inc(t2_masked, 1)
                dve.wait_ge(t2_hi, blk + 1)
                V.tensor_tensor(t2p[:, 1, :], t2f[:, :], f32(t2p[:, 0, :]), ALU.subtract).then_inc(t2_lo, 1)

            def x2(blk, par, last=False):
                dve.wait_ge(x2_psum, blk + 1)
                for k in range(KD):
                    if last and k:
                        dve.wait_ge(x2_psum, blk + 1 + k)
                    V.tensor_tensor(x1[:, par, k, :], x2_bank[k][:, :], x1[:, par, k, :], ALU.add).then_inc(x2_full, 1)

            def x2lo(blk, par, half, own=0):
                dve.wait_ge(x2_hi, 2 * blk + half + 1)
                for k in range(KD):
                    last = V.tensor_tensor(x2_part(1, own, k), half_tokens(par, k, half), f32(x2_part(0, own, k)),
                                           ALU.subtract)
                last.then_inc(x2_lo, 1)

            def wait_tables(blk, half, own, landed):
                if own:
                    dve.wait_ge(last_landed, LAST_LOADS)
                else:
                    dve.wait_ge(landed, 16 * HR * (2 * blk + half + 1))

            def x3_(blk, half, own=0, bank_of=x3_bank):
                dve.wait_ge(x3_moved, 2 * blk + half + 1)
                wait_tables(blk, half, own, bias_landed)
                lo = x3lo_own[own]
                V.tensor_tensor(lo, lo, bias_of[own].rearrange("p t c -> p (t c)"),
                                ALU.add).then_inc(x3_biased, 1)
                dve.wait_ge(x3_biased, 2 * blk + half + 1)
                dve.wait_ge(out_rows, 2 * blk)
                even, odd = bank_of[half]
                V.tensor_tensor(x3[0:SEQ, half, :], even[0:SEQ, :], lo[0:SEQ], ALU.add)
                V.tensor_tensor(x3[SEQ:P, half, :], odd[SEQ:P, :], lo[SEQ:P], ALU.add).then_inc(x3_rows, 1)

            def x3t(blk, half, own=0, bank_of=x3t_bank):
                dve.wait_ge(x3t_hi, 2 * blk + half + 1)
                V.tensor_tensor(x3p_own[own][:, :, :, 1, :],
                                rows_of(bank_of[half][:, :].rearrange("p (k t) -> p k t", k=KD)),
                                f32(x3p_own[own][:, :, :, 0, :]), ALU.subtract).then_inc(x3t_lo, 1)

            def z_(blk, half, own=0, bank_of=z_bank):
                dve.wait_ge(z_lo, 2 * blk + half + 1)
                for t in range(PAIRS):
                    v, sums = z_parts(t, own, bank_of[half])
                    last = V.tensor_tensor(v, sums[:, :, 0, :], v, ALU.add)
                last.then_inc(z_rows, 1)

            def zt_bias(blk, half, own=0, bank_of=zt_bank):
                dve.wait_ge(zt_psum, 2 * blk + half + 1)
                b = row_cols[:, KD, bass.ds(blk * BR + half * HR, HR)].unsqueeze(2).broadcast_to([P, HR, SEQ])
                v = zb_of_own[own].rearrange("p (r c) -> p r c", c=SEQ)
                parts = bank_of[half][:, :].rearrange("p (r s c) -> p r s c", s=2, c=SEQ)
                V.tensor_tensor(v, parts[:, :, 1, :], b, ALU.add).then_inc(zt_lo_sum, 1)
                dve.wait_ge(zt_lo_sum, 2 * blk + half + 1)
                V.tensor_tensor(v, parts[:, :, 0, :], v, ALU.add).then_inc(zt_biased, 1)

            def zt(blk, half, own=0):
                dve.wait_ge(zt_hi, 2 * blk + half + 1)
                V.scalar_tensor_tensor(out=pad_z(1, own), in0=zb_of_own[own].rearrange("p (r c) -> p r c", c=SEQ),
                                       scalar=0.0, in1=f32(pad_z(0, own)), op0=ALU.max, op1=ALU.subtract).then_inc(zt_lo, 1)

            def y_(blk, half, bank_of=y_bank):
                dve.wait_ge(y_psum, 2 * blk + half + 1)
                dve.wait_ge(y_base, 2 * blk + half + 1)
                V.tensor_tensor(y[:, half, :], bank_of[half][:, :], y[:, half, :], ALU.add).then_inc(y_rows, 1)

            def stat(blk, half):
                dve.wait_ge(y_rows, 2 * blk + half + 1)
                for t in range(PAIRS):
                    last = V.bn_stats(stats[:, t, :], y[:, half, t * D:(t + 1) * D])
                last.then_inc(y_stats, 1)

            def aggregate(half):
                for t in range(PAIRS):
                    last = V.bn_aggr(mv[:, half, t, :], stats[:, t, :])
                last.then_inc(y_moments, 1)

            def normalize(blk, half):
                dve.wait_ge(y_rstd, 2 * blk + half + 1)
                for t in range(PAIRS):
                    v = y[:, half, t * D:(t + 1) * D]
                    last = V.tensor_scalar(v, v, mv[:, half, t, 0:1], rstd[:, half, t:t + 1], ALU.subtract, ALU.mult)
                last.then_inc(y_norm, 1)

            def t0(blk):
                dve.wait_ge(t0_psum, blk + 1)
                masked(tf[:, :], t0_bank, 0, blk).then_inc(t0_masked, 1)

            def t0lo(blk):
                dve.wait_ge(t0_hi, blk + 1)
                V.tensor_tensor(t0p[SEQ:P, :], tf[SEQ:P, :], f32(t0p[SEQ:P, :]), ALU.subtract).then_inc(t0_lo, 1)

            def x1_sum(blk, par):
                dve.wait_ge(xe_ready, blk + 1)
                for k in range(KD):
                    dve.wait_ge(x1_psum, 2 * blk + k + 1)
                    V.tensor_tensor(x1[:, par, k, :], x1_bank[k][:, :], x_in[:, k, :], ALU.add).then_inc(x1_full, 1)

            def x1lo(blk, par):
                dve.wait_ge(x1_hi, blk + 1)
                V.tensor_tensor(x1p[:, par, 1, :, :].rearrange("p k t -> p (k t)"),
                                x1[:, par, :, :].rearrange("p k t -> p (k t)"),
                                f32(x1p[:, par, 0, :, :]).rearrange("p k t -> p (k t)"),
                                ALU.subtract).then_inc(x1_lo, 1)

            def t1(blk):
                dve.wait_ge(t0_lo, blk + 1)
                dve.wait_ge(t1_psum, blk + 1)
                masked(tf[:, :], t1_bank, 1, blk).then_inc(t1_masked, 1)

            def t1lo(blk):
                dve.wait_ge(t1_hi, blk + 1)
                V.tensor_tensor(t1p[:, 1, :], tf[:, :], f32(t1p[:, 0, :]), ALU.subtract).then_inc(t1_lo, 1)

            def factor(j):
                src, dst, g = FACTORS[j]
                dve.wait_ge(factor_hi, j + 1)
                q = slice(g * CG, (g + 1) * CG)
                V.tensor_tensor(dst[q], src[q], f32(dst[q]), ALU.subtract).then_inc(factor_split, 1)

            def first_front():
                split_lo(0)
                dve.wait_ge(xh_ready, 1)
                V.tensor_tensor(x1p[:, 0, 1, :, :].rearrange("p k t -> p (k t)"),
                                x_in[:, :, :].rearrange("p k t -> p (k t)"),
                                f32(x1p[:, 0, 0, :, :]).rearrange("p k t -> p (k t)"),
                                ALU.subtract).then_inc(xl_ready, 1)
                make_masks()
                factor(0)
                factor(1)
                dve.wait_ge(masks_made, 1)
                t0(0)
                t0lo(0)
                add_to(2)
                x1_sum(0, 0)
                split_lo(2)
                x1lo(0, 0)
                factor(2)
                factor(3)
                t1(0)
                t1lo(0)
                add_to(4)
                add_to(5)

            def step(n, par, main, tail, front):
                blk_t, blk_f = n - 1, n + 1
                if not main:
                    first_front()
                    return
                h(n, 0)
                if tail:
                    t2(blk_t)
                h(n, 1)
                if tail:
                    x2(blk_t, 1 - par)
                    x2lo(blk_t, 1 - par, 0)
                h(n, 2)
                if tail:
                    x3_(blk_t, 0)
                h(n, 3)
                if tail:
                    x3t(blk_t, 0)
                    x2lo(blk_t, 1 - par, 1)
                    z_(blk_t, 0)
                    zt_bias(blk_t, 0)
                h(n, 4)
                if first_block(n):
                    late(4)
                if tail:
                    zt(blk_t, 0)
                    y_(blk_t, 0)
                    stat(blk_t, 0)
                    x3_(blk_t, 1)
                h(n, 5)
                if first_block(n):
                    late(5)
                if tail:
                    dve.wait_ge(y_stats, 2 * blk_t + 1)
                    x3t(blk_t, 1)
                    aggregate(0)
                if front:
                    dve.wait_ge(t1_lo, blk_f)
                    t0(blk_f)
                    t0lo(blk_f)
                h(n, 6)
                if tail:
                    z_(blk_t, 1)
                    zt_bias(blk_t, 1)
                if front:
                    if tail:
                        dve.wait_ge(x2_lo, 2 * blk_t + 2)
                    x1_sum(blk_f, 1 - par)
                if tail:
                    zt(blk_t, 1)
                    normalize(blk_t, 0)
                if front:
                    x1lo(blk_f, 1 - par)
                h(n, 7)
                if front:
                    t1(blk_f)
                if tail:
                    y_(blk_t, 1)
                    stat(blk_t, 1)
                    dve.wait_ge(y_stats, 2 * blk_t + 2)
                if front:
                    t1lo(blk_f)
                if tail:
                    aggregate(1)
                if tail and front:
                    normalize(blk_t, 1)

            def last_tail(blk, par):
                t2(blk)
                normalize(blk - 1, 1)
                x2(blk, par, True)
                for half in range(2):
                    x2lo(blk, par, half, half)
                for half in range(2):
                    x3_(blk, half, half, last_x3_bank)
                for half in range(2):
                    x3t(blk, half, half, last_x3t_bank)
                for half in range(2):
                    z_(blk, half, half, last_z_bank)
                for half in range(2):
                    zt_bias(blk, half, half, last_zt_bank)
                for half in range(2):
                    zt(blk, half, half)
                y_(blk, 0, last_y_bank)
                stat(blk, 0)
                dve.wait_ge(y_stats, 2 * blk + 1)
                aggregate(0)
                y_(blk, 1, last_y_bank)
                stat(blk, 1)
                dve.wait_ge(y_stats, 2 * blk + 2)
                aggregate(1)
                normalize(blk, 0)
                normalize(blk, 1)
                dve.wait_ge(y_norm, 2 * blk + 2)
                dve.wait_ge(last_landed, LAST_LOADS)
                V.tensor_tensor(y[:, 1, :], y[:, 1, :], gains_of[1].rearrange("p t c -> p (t c)"),
                                ALU.mult).then_inc(last_gained, 1)
                dve.wait_ge(last_gained, 1)
                dve.wait_ge(x3_base, 2 * blk + 2)
                V.tensor_tensor(y[:, 1, :], y[:, 1, :], x3[:, 1, :], ALU.add).then_inc(last_rows, 1)

            steps(dve, step, last_tail)

        @block.gpsimd
        def _(pool):
            G = nc.gpsimd
            G.iota(group_i[:, 2:3], pattern=[[0, 1]], base=0, channel_multiplier=1).then_inc(consts_made, 1)
            G.memset(ident[:, :], 0.0).then_inc(ident_made, 1)
            pool.wait_ge(ident_made, 1)
            G.affine_select(out=ident[:, :], in_=ident[:, :], compare_op=ALU.not_equal, fill=1.0, base=0,
                            pattern=[[-1, P]], channel_multiplier=1).then_inc(ident_made, 1)
            G.memset(f32(zpad[:, :, :]), 0.0)
            G.memset(eps[:, :], EPS)
            G.memset(minus_half[:, :], -0.5).then_inc(consts_made, 1)
            pool.wait_ge(consts_made, 2)

            def split_lo(c):
                pool.wait_ge(chunk_hi, c + 1)
                G.tensor_tensor(CHUNKS[c](1), staged(c), f32(CHUNKS[c](0)), ALU.subtract).then_inc(chunk_split_g, 1)

            def x_lo(blk, par):
                pool.wait_ge(xh_ready, blk + 1)
                G.tensor_tensor(x1p[:, par, 1, :, :].rearrange("p k t -> p (k t)"),
                                x_in[:, :, :].rearrange("p k t -> p (k t)"),
                                f32(x1p[:, par, 0, :, :]).rearrange("p k t -> p (k t)"),
                                ALU.subtract).then_inc(xl_ready, 1)

            def x_embedded(blk):
                pool.wait_ge(xl_ready, blk + 1)
                for k in range(KD):
                    e = row_cols[:, k, bass.ds(blk * BR, BR)].unsqueeze(2).broadcast_to([P, BR, SEQ])
                    v = x_in[:, k, :].rearrange("p (r c) -> p r c", c=SEQ)
                    last = G.tensor_tensor(v, v, e, ALU.add)
                last.then_inc(xe_ready, 1)

            def base(blk, half, own=0):
                done = 2 * blk + half
                pool.wait_ge(x3_rows, done + 1)
                if own:
                    pool.wait_ge(last_landed, LAST_LOADS)
                else:
                    pool.wait_ge(adds_landed, 16 * HR * (done + 1))
                pool.wait_ge(out_stored[half], 16 * blk)
                x3v = x3[:, half, :].rearrange("p (t c) -> p t c", c=D)
                G.tensor_tensor(y[:, half, :].rearrange("p (t c) -> p t c", c=D), x3v, bases_of[own][:, :, 0:D],
                                ALU.add).then_inc(y_base, 1)
                pool.wait_ge(x3t_psum, done + 1)
                pool.wait_ge(y_base, done + 1)
                G.tensor_tensor(x3v, x3v, bases_of[own][:, :, D:2 * D], ALU.add).then_inc(x3_base, 1)

            def inverse_deviation(blk, half):
                pool.wait_ge(y_moments, 2 * blk + half + 1)
                G.tensor_tensor(rstd[:, half, :], mv[:, half, :, 1], eps[:, :], ALU.add).then_inc(var_eps, 1)
                pool.wait_ge(var_eps, 2 * blk + half + 1)
                G.tensor_tensor(rstd[:, half, :], rstd[:, half, :], minus_half[:, :], ALU.pow).then_inc(y_rstd, 1)

            def finish(blk, half):
                done = 2 * blk + half
                pool.wait_ge(y_norm, done + 1)
                pool.wait_ge(gains_landed, 16 * HR * (done + 1))
                G.tensor_tensor(y[:, half, :], y[:, half, :], gains[:, :, :].rearrange("p t c -> p (t c)"),
                                ALU.mult).then_inc(y_gained, 1)
                pool.wait_ge(y_gained, done + 1)
                pool.wait_ge(x3_base, done + 1)
                G.tensor_tensor(y[:, half, :], y[:, half, :], x3[:, half, :], ALU.add).then_inc(out_rows, 1)

            def step(n, par, main, tail, front):
                blk_t, blk_f = n - 1, n + 1
                if not main:
                    split_lo(SPLIT_G[0])
                    pool.wait_ge(emb_made, 1)
                    x_embedded(blk_f)
                    split_lo(SPLIT_G[1])
                elif front:
                    x_lo(blk_f, 1 - par)
                    x_embedded(blk_f)
                if first_block(n):
                    for c in SPLIT_G[2:]:
                        split_lo(c)
                if tail:
                    base(blk_t, 0)
                    base(blk_t, 1)
                if tail:
                    for half in range(2):
                        inverse_deviation(blk_t, half)
                        finish(blk_t, half)

            def last_tail(blk, par):
                pool.wait_ge(h_psum, 8 * BLOCKS)
                G.memset(f32(zpads[1]), 0.0).then_inc(pads_cleared, 1)
                base(blk, 0, 0)
                base(blk, 1, 1)
                inverse_deviation(blk, 0)
                inverse_deviation(blk, 1)
                finish(blk, 0)

            steps(pool, step, last_tail)


def _layouts(i):
    import numpy as np
    c = np.ascontiguousarray
    copies = lambda a: c(np.tile(a, (3 * CG // RANK, 1)))
    tiles = lambda a: a.reshape(-1, P, a.shape[-1]).transpose(1, 0, 2).reshape(P, -1)
    la = i["L0_cond_lora_A"].reshape(LANGS * RANK, D).T
    la = np.concatenate([la, la], 1)
    lb = i["L0_cond_lora_B"].transpose(0, 2, 1).reshape(LANGS * RANK, D)
    lb = np.concatenate([lb, lb], 0)
    ewia = i["L1_cond_experts_wi_a"].reshape(EXPERTS * RANK, D).T
    ewib = i["L1_cond_experts_wi_b"].transpose(0, 2, 1).reshape(EXPERTS * RANK, F)
    ewoa = i["L1_cond_experts_wo_a"].reshape(EXPERTS * RANK, F).T
    ewob = i["L1_cond_experts_wo_b"].transpose(0, 2, 1).reshape(EXPERTS * RANK, D)
    sub = i["L2_cond_weight"].transpose(2, 0, 1).reshape(D, EXPERTS * D)
    down = i["L3_cond_down_w"].transpose(1, 0, 2).reshape(D, PROFILES * BOTTLE)
    up = i["L3_cond_up_w"].transpose(1, 0, 2).reshape(BOTTLE, PROFILES * D)
    wi, wo = i["L1_cond_wi"].T, tiles(i["L1_cond_wo"].T)
    w = np.concatenate([tiles(la), lb, tiles(ewia), ewob, ewib, tiles(wi[:, :512]), tiles(ewoa), wo[:, :CHUNK],
                        tiles(wi[:, 512:]), wo[:, CHUNK:], tiles(sub), tiles(down), up], 1)
    w = w.reshape(P, -1, CHUNK).transpose(1, 0, 2)
    return {
        "xT": c(i["x"].reshape(TOKENS, KD, P).transpose(2, 1, 0)),
        "lang": c(i["itok_B_0_3"].reshape(ROWS)), "expert": c(i["itok_B_0_7"].reshape(ROWS)),
        "profile": c(i["itok_B_0_6"].reshape(ROWS)),
        "lang_emb": c(i["L0_cond_lang_embed"]),
        "common_small": copies(np.concatenate([i["L1_cond_common_wi_a"], i["L1_cond_common_wo_b"].T], 1)),
        "common_wi_bT": copies(i["L1_cond_common_wi_b"].T), "common_wo_a": copies(i["L1_cond_common_wo_a"]),
        "weights": c(w), "sub_b": c(i["L2_cond_bias"]), "down_b": c(i["L3_cond_down_b"]),
        "prof_adds": c(np.concatenate([i["L3_cond_up_b"], i["L3_cond_ln_b"]], 1)),
        "prof_g": c(i["L3_cond_ln_g"]),
    }


def kernel(**inputs):
    import numpy as np
    import concourse.bacc as bacc
    from concourse.bass_utils import run_bass_kernel_spmd

    arrays = _layouts({k: np.asarray(v) for k, v in inputs.items()})
    nc = bacc.Bacc("TRN2", target_bir_lowering=False, num_devices=1)
    args = [nc.dram_tensor(f"in_{k}", a.shape, mybir.dt.from_np(a.dtype), kind="ExternalInput").ap()
            for k, a in arrays.items()]
    out = nc.dram_tensor("out_rows", (TOKENS, D), F32, kind="ExternalOutput").ap()
    build(nc, *args, out)
    r = run_bass_kernel_spmd(nc, [{f"in_{k}": a for k, a in arrays.items()}], core_ids=[0])
    return r.results[0]["out_rows"].reshape(ROWS, SEQ, D)
```
